# Optimizing a Trainium2 kernel written in Bass

```python
import numpy as np
import jax
import jax.numpy as jnp

def _softmax(x, axis=-1):
    return jax.nn.softmax(x, axis=axis)

def _gelu(x):
    return jax.nn.gelu(x, approximate=True)

def _silu(x):
    return jax.nn.silu(x)

def _sigmoid(x):
    return jax.nn.sigmoid(x)

def _layernorm(x, axis=-1, eps=1e-05):
    m = jnp.mean(x, axis=axis, keepdims=True)
    v = jnp.var(x, axis=axis, keepdims=True)
    return (x - m) / jnp.sqrt(v + eps)

def _scatter_add(tgt, idx, src, axis=0):
    return tgt.at[idx].add(src)

def _segment_sum(src, seg, n):
    return jax.ops.segment_sum(src, seg, n)
kernel_name = 'mk_gnn_resnorm_d1_gnn_r16_466f2a'

def setup_inputs(seed: int=0):
    np.random.seed(seed)
    _w = jnp.asarray

    def _rec_inputs():
        import jax
        import jax.numpy as jnp
        _gk = jax.random.key(seed)
        x = -0.000202 + 1 * jax.random.normal(jax.random.fold_in(_gk, 1), (3125, 128), jnp.float32)
        src = jax.random.randint(jax.random.fold_in(_gk, 2), (100000,), 0, 3125, jnp.int32)
        dst = jax.random.randint(jax.random.fold_in(_gk, 3), (100000,), 0, 3125, jnp.int32)
        _o = jnp.argsort(dst, stable=True)
        src = src[_o]
        dst = dst[_o]
        edge_type_5 = jax.random.randint(jax.random.fold_in(_gk, 12), (100000,), 0, 5, jnp.int32)
        return (x, src, dst, edge_type_5)
    x, src, dst, edge_type_5 = _rec_inputs()

    def _L0_gnn_setup():
        import jax, jax.numpy as jnp
        import numpy as np
        N = 3125
        E = 40000
        HIDDEN = 128
        R = 5
        HEADS = 8
        HEAD_DIM = HIDDEN // HEADS
        LN_EPS = 1e-05

        def _fused_forward(node_embeddings, W_Q, W_K, W_V, attn_bias, out_proj_w, out_proj_b, ln_gamma, ln_beta, edge_index, edge_types):
            src, dst = (edge_index[0], edge_index[1])
            n = node_embeddings.shape[0]
            x_src = node_embeddings[src]
            x_dst = node_embeddings[dst]
            scale = HEAD_DIM ** 0.5
            NEG = jnp.float32(-1000000000.0)
            out = jnp.zeros((n, HEADS, HEAD_DIM), dtype=node_embeddings.dtype)
            for r in range(R):
                mask = edge_types == r
                q = jnp.einsum('eh,khd->ekd', x_dst, W_Q[r])
                k = jnp.einsum('eh,khd->ekd', x_src, W_K[r])
                v = jnp.einsum('eh,khd->ekd', x_src, W_V[r])
                logits = (q * k).sum(-1) / scale + attn_bias[r][None, :]
                masked_logits = jnp.where(mask[:, None], logits, NEG)
                max_v = jax.ops.segment_max(masked_logits, dst, num_segments=n)
                max_v = jnp.maximum(max_v, NEG)
                exp_l = jnp.where(mask[:, None], jnp.exp(masked_logits - max_v[dst]), 0.0)
                sum_exp = jax.ops.segment_sum(exp_l, dst, num_segments=n)
                attn = exp_l / (sum_exp[dst] + 1e-12)
                out = out + jax.ops.segment_sum(attn[:, :, None] * v, dst, num_segments=n)
            out = out.reshape(n, HIDDEN)
            out = out @ out_proj_w.T + out_proj_b
            h = out + node_embeddings
            mu = h.mean(-1, keepdims=True)
            var = ((h - mu) ** 2).mean(-1, keepdims=True)
            return (h - mu) / jnp.sqrt(var + LN_EPS) * ln_gamma + ln_beta
        key = jax.random.key(seed)
        ks = jax.random.split(key, 10)
        bound = float(np.sqrt(6.0 / (HIDDEN + HEAD_DIM)))
        pbound = float(np.sqrt(1.0 / HIDDEN))
        return {'node_embeddings': jax.random.normal(ks[0], (N, HIDDEN), dtype=jnp.float32), 'edge_index': jax.random.randint(ks[1], (2, E), 0, N, dtype=jnp.int64), 'edge_types': jax.random.randint(ks[2], (E,), 0, R, dtype=jnp.int64), 'W_Q': jax.random.uniform(ks[3], (R, HEADS, HIDDEN, HEAD_DIM), minval=-bound, maxval=bound, dtype=jnp.float32), 'W_K': jax.random.uniform(ks[4], (R, HEADS, HIDDEN, HEAD_DIM), minval=-bound, maxval=bound, dtype=jnp.float32), 'W_V': jax.random.uniform(ks[5], (R, HEADS, HIDDEN, HEAD_DIM), minval=-bound, maxval=bound, dtype=jnp.float32), 'attn_bias': jnp.zeros((R, HEADS), dtype=jnp.float32), 'out_proj_w': jax.random.uniform(ks[6], (HIDDEN, HIDDEN), minval=-pbound, maxval=pbound, dtype=jnp.float32), 'out_proj_b': jax.random.uniform(ks[7], (HIDDEN,), minval=-pbound, maxval=pbound, dtype=jnp.float32), 'ln_gamma': jnp.ones((HIDDEN,), dtype=jnp.float32), 'ln_beta': jnp.zeros((HIDDEN,), dtype=jnp.float32)}
    _L0_gnn_all = _L0_gnn_setup()
    _L0_gnn_in = {k: v for k, v in _L0_gnn_all.items() if k in ('W_Q', 'W_K', 'W_V', 'attn_bias', 'out_proj_w', 'out_proj_b', 'ln_gamma', 'ln_beta')}
    del _L0_gnn_all
    return {'x': x, 'src': src, 'dst': dst, 'edge_type_5': edge_type_5, 'L0_gnn_W_Q': _L0_gnn_in['W_Q'], 'L0_gnn_W_K': _L0_gnn_in['W_K'], 'L0_gnn_W_V': _L0_gnn_in['W_V'], 'L0_gnn_attn_bias': _L0_gnn_in['attn_bias'], 'L0_gnn_out_proj_w': _L0_gnn_in['out_proj_w'], 'L0_gnn_out_proj_b': _L0_gnn_in['out_proj_b'], 'L0_gnn_ln_gamma': _L0_gnn_in['ln_gamma'], 'L0_gnn_ln_beta': _L0_gnn_in['ln_beta']}

def reference(x, src, dst, edge_type_5, L0_gnn_W_Q, L0_gnn_W_K, L0_gnn_W_V, L0_gnn_attn_bias, L0_gnn_out_proj_w, L0_gnn_out_proj_b, L0_gnn_ln_gamma, L0_gnn_ln_beta):
    import jax
    import jax.numpy as jnp

    def _L0_gnn_ref(node_embeddings, edge_index, edge_types, W_Q, W_K, W_V, attn_bias, out_proj_w, out_proj_b, ln_gamma, ln_beta):
        import jax, jax.numpy as jnp
        import numpy as np
        N = 3125
        E = 40000
        HIDDEN = 128
        R = 5
        HEADS = 8
        HEAD_DIM = HIDDEN // HEADS
        LN_EPS = 1e-05

        def _fused_forward(node_embeddings, W_Q, W_K, W_V, attn_bias, out_proj_w, out_proj_b, ln_gamma, ln_beta, edge_index, edge_types):
            src, dst = (edge_index[0], edge_index[1])
            n = node_embeddings.shape[0]
            x_src = node_embeddings[src]
            x_dst = node_embeddings[dst]
            scale = HEAD_DIM ** 0.5
            NEG = jnp.float32(-1000000000.0)
            out = jnp.zeros((n, HEADS, HEAD_DIM), dtype=node_embeddings.dtype)
            for r in range(R):
                mask = edge_types == r
                q = jnp.einsum('eh,khd->ekd', x_dst, W_Q[r])
                k = jnp.einsum('eh,khd->ekd', x_src, W_K[r])
                v = jnp.einsum('eh,khd->ekd', x_src, W_V[r])
                logits = (q * k).sum(-1) / scale + attn_bias[r][None, :]
                masked_logits = jnp.where(mask[:, None], logits, NEG)
                max_v = jax.ops.segment_max(masked_logits, dst, num_segments=n)
                max_v = jnp.maximum(max_v, NEG)
                exp_l = jnp.where(mask[:, None], jnp.exp(masked_logits - max_v[dst]), 0.0)
                sum_exp = jax.ops.segment_sum(exp_l, dst, num_segments=n)
                attn = exp_l / (sum_exp[dst] + 1e-12)
                out = out + jax.ops.segment_sum(attn[:, :, None] * v, dst, num_segments=n)
            out = out.reshape(n, HIDDEN)
            out = out @ out_proj_w.T + out_proj_b
            h = out + node_embeddings
            mu = h.mean(-1, keepdims=True)
            var = ((h - mu) ** 2).mean(-1, keepdims=True)
            return (h - mu) / jnp.sqrt(var + LN_EPS) * ln_gamma + ln_beta
        return _fused_forward(node_embeddings, W_Q, W_K, W_V, attn_bias, out_proj_w, out_proj_b, ln_gamma, ln_beta, edge_index, edge_types)
    edge_index = jnp.stack([src, dst])
    x = _layernorm(x + _L0_gnn_ref(x, edge_index, edge_type_5, L0_gnn_W_Q, L0_gnn_W_K, L0_gnn_W_V, L0_gnn_attn_bias, L0_gnn_out_proj_w, L0_gnn_out_proj_b, L0_gnn_ln_gamma, L0_gnn_ln_beta), axis=-1)
    return x

_drawn_inputs = setup_inputs


def setup_inputs(seed=0):
    import zlib

    import numpy as np

    out = dict(_drawn_inputs(seed))
    spreads = {'L0_gnn_attn_bias': (0.0, 0.8),
     'L0_gnn_ln_gamma': (1.0, 0.2),
     'L0_gnn_ln_beta': (0.0, 0.1)}
    factors = {'L0_gnn_out_proj_b': 2.891}
    for name, (base, spread) in spreads.items():
        noise = np.random.default_rng([zlib.crc32(name.encode()), seed]).standard_normal(out[name].shape)
        drawn = base * np.exp(spread * noise) if base else spread * noise
        out[name] = jnp.asarray(drawn.astype(out[name].dtype))
    for name, factor in factors.items():
        out[name] = (out[name] * factor).astype(out[name].dtype)
    return out
```

```python
import concourse.bass as bass
from concourse import mybir
from contextlib import ExitStack

N = 3125
E = 100000
R = 5
H = 8
D = 16
C = 128
NB = 25
NT = 782
KEYS = N * R
PAD_ROW = KEYS
DUP_ROW = KEYS + 128
ROWS = 16128
QW = C + H
AW = C + H
NEG = -1.0e9
FAR = -1.0e30
EPS = 1e-5

F32 = mybir.dt.float32
I32 = mybir.dt.int32
U32 = mybir.dt.uint32
ALU = mybir.AluOpType
ACT = mybir.ActivationFunctionType
AX = mybir.AxisListType


class Step:

    def __init__(self, sems, inc):
        self.sems = sems
        self.inc = inc

    def wait(self, eng, times):
        if len(self.sems) == 1:
            eng.wait_ge(self.sems[0], times * self.inc)
        else:
            eng.wait_ge(self.sems[(times - 1) % len(self.sems)], ((times - 1) // len(self.sems) + 1) * self.inc)

    def wait_all(self, eng, times):
        for t in range(max(times - len(self.sems), 0), times):
            self.wait(eng, t + 1)

    def end(self, ins, i):
        ins.then_inc(self.sems[0] if len(self.sems) == 1 else self.sems[i % len(self.sems)], self.inc)


class Queues:

    def __init__(self, nc, ctx):
        self.nc = nc
        self.ctx = ctx
        self.steps = {}
        self.tick = ctx.enter_context(nc.semaphore("tick"))
        self.lists = {"sync": [], "scalar": [], "vector": [], "gpsimd": [], "tensor": []}

    def step(self, name, inc):
        if name not in self.steps:
            inc, n = inc if isinstance(inc, tuple) else (inc, 1)
            self.steps[name] = Step([self.ctx.enter_context(self.nc.semaphore(f"s_{name}_{k}")) for k in range(n)], inc)
        return self.steps[name]

    def loop(self, count, body, rolled):
        for _, name, inc, _, _ in body:
            self.step(name, inc)
        for key in self.lists:
            mine = [b for b in body if b[0] == key]
            if mine:
                self.lists[key].append((count, mine, rolled))

    def once(self, eng, name, inc, after, emit):
        self.step(name, inc)
        self.lists[eng].append((1, [(eng, name, inc, after, emit)], False))

    def turn(self, eng, mine, i, key, rolled):
        for _, name, inc, after, emit in mine:
            for a in after:
                if len(a) == 3:
                    self.steps[a[0]].wait_all(eng, a[2])
                elif a[1] == 0 or not isinstance(i, int) or i + 1 + a[1] > 0:
                    self.steps[a[0]].wait(eng, i + (1 + a[1]))
            if key == "gpsimd" and rolled:
                eng.sem_inc(self.tick, 1)
            self.steps[name].end(emit(eng, i), i)

    def emit(self, key, eng):
        for count, mine, rolled in self.lists[key]:
            if rolled:
                self.turn(eng, mine, 0, key, rolled)
                with eng.Fori(1, count) as i:
                    self.turn(eng, mine, i, key, rolled)
            else:
                for i in range(count):
                    self.turn(eng, mine, i, key, rolled)


def build(nc, x, src, dst, typ, wq, wk, wv, bias, wo, bo, gamma, beta, out):
    ctx = ExitStack()
    with ctx:
        def sb(name, shape, dt=F32):
            return ctx.enter_context(nc.sbuf_tensor(name, shape, dt))

        def ps(name, shape, dt=F32):
            return ctx.enter_context(nc.psum_tensor(name, shape, dt))

        KV = nc.dram_tensor("KVtab", [NB * 640, 2 * C], F32).ap()
        QT = nc.dram_tensor("Qtab", [NB * 640, QW], F32).ap()
        MX = nc.dram_tensor("MXtab", [ROWS, H], F32).ap()
        ACC = nc.dram_tensor("ACCtab", [ROWS, AW], F32).ap()

        xs = sb("xs", [128, NB, C])
        xT = sb("xT", [128, NB * 128])
        aggT = sb("aggT", [128, NB * 128])
        W = sb("W", [128, 3, R, C])
        woS = sb("woS", [128, C])
        woT = sb("woT", [128, C])
        bb = sb("bb", [128, R, H])
        bob = sb("bob", [128, C])
        gab = sb("gab", [128, C])
        beb = sb("beb", [128, C])
        ident = sb("ident", [128, 128])
        tri = sb("tri", [128, 128])
        pid = sb("pid", [128, 1])
        nat = sb("nat", [112, 3, 7, 128], I32)
        natf = sb("natf", [112, 3, 7, 128])
        keyf = sb("keyf", [128, 784])
        kvf = sb("kvf", [128, 784])
        keyi = sb("keyi", [128, 784], U32)
        kvi = sb("kvi", [128, 784], U32)
        stg = sb("stg", [128, 2, R, 2 * C])
        stq = sb("stq", [128, 2, R, QW])
        pp = [ps(f"pp{i}", [128, 512]) for i in range(8)]

        q = Queues(nc, ctx)
        once, loop = q.once, q.loop

        once("gpsimd", "id0", 1, [], lambda e, i: e.memset(ident[:, :], 0.0))
        once("gpsimd", "id", 1, [("id0", None, 1)], lambda e, i: e.affine_select(
            out=ident[:, :], in_=ident[:, :], compare_op=ALU.not_equal, fill=1.0, base=0,
            pattern=[[-1, 128]], channel_multiplier=1))
        once("gpsimd", "tri0", 1, [], lambda e, i: e.memset(tri[:, :], 1.0))
        once("gpsimd", "tri", 1, [("tri0", None, 1)], lambda e, i: e.affine_select(
            out=tri[:, :], in_=tri[:, :], compare_op=ALU.is_gt, fill=0.0, base=0,
            pattern=[[-1, 128]], channel_multiplier=1))
        once("gpsimd", "pid", 1, [], lambda e, i: e.iota(
            pid[:, :], [[0, 1]], base=0, channel_multiplier=1, allow_small_or_imprecise_dtypes=True))
        once("vector", "nz", 1, [], lambda e, i: e.memset(nat[:, :, 6, :], 0))
        once("vector", "xz", 1, [], lambda e, i: e.memset(xs[:, 24, :], 0.0))
        for k, a in enumerate((dst, src, typ)):
            for c in range(6):
                once("sync", f"nat{k}", 16, [], lambda e, i, k=k, a=a, c=c: e.dma_start(
                    nat[:, k, c, :], a[c * 14336:(c + 1) * 14336].rearrange("(t p) -> t p", p=128)))
            once("sync", f"nat{k}", 16, [("nz", None, 1)], lambda e, i, k=k, a=a: e.dma_start(
                nat[0:109, k, 6, :], a[6 * 14336:6 * 14336 + 109 * 128].rearrange("(t p) -> t p", p=128)))
            once("sync", f"nat{k}", 16, [("nz", None, 1)], lambda e, i, k=k, a=a: e.dma_start(
                nat[109:110, k, 6, 0:32], a[781 * 128:E].rearrange("(t p) -> t p", t=1)))
        once("scalar", "xl", 16, [], lambda e, i: e.dma_start(
            xs[:, 0:24, :], x[0:3072, :].rearrange("(b p) c -> p b c", p=128)))
        once("scalar", "xl", 16, [("xz", None, 1)], lambda e, i: e.dma_start(xs[0:53, 24, :], x[3072:N, :]))
        for k, a in enumerate((wq, wk, wv)):
            for r in range(R):
                once("scalar", "wl", 16, [], lambda e, i, k=k, a=a, r=r: e.dma_start(
                    W[:, k, r, :].rearrange("p (k d) -> p k d", d=D), a[r].rearrange("k h d -> h k d")))
        once("scalar", "wl", 16, [], lambda e, i: e.dma_start(woS[:, :], wo))
        once("scalar", "wl", 16, [], lambda e, i: e.dma_start(
            bb[:, :, :].rearrange("p r h -> p (r h)"),
            bias.rearrange("r h -> (r h)").partition_broadcast(128)))
        for dst_, a in ((bob, bo), (gab, gamma), (beb, beta)):
            once("scalar", "wl", 16, [], lambda e, i, d=dst_, a=a: e.dma_start(d[:, :], a.partition_broadcast(128)))

        once("vector", "natf", 1, [("nat0", None, 8), ("nat1", None, 8), ("nat2", None, 8)],
             lambda e, i: e.tensor_copy(natf[:, :, :, :], nat[:, :, :, :]))
        once("vector", "natk", 1, [("natf", None, 1)], lambda e, i: e.scalar_tensor_tensor(
            natf[:, 0, :, :], natf[:, 0, :, :], 5.0, natf[:, 2, :, :], ALU.mult, ALU.add))
        once("vector", "natv", 1, [("natk", None, 1)], lambda e, i: e.scalar_tensor_tensor(
            natf[:, 1, :, :], natf[:, 1, :, :], 5.0, natf[:, 2, :, :], ALU.mult, ALU.add))
        for k in range(2):
            for c in range(7):
                once("tensor", f"kt{k}", 1, [("natv", None, 1), ("id", None, 1)],
                     lambda e, i, k=k, c=c: e.transpose(
                         pp[2 * k + c // 4][:, (c % 4) * 112:(c % 4) * 112 + 112], natf[:, k, c, :],
                         ident[0:112, 0:112]))
        for k, (f, w) in enumerate(((keyf, keyi), (kvf, kvi))):
            once("vector", f"kf{k}", 1, [(f"kt{k}", None, 7)],
                 lambda e, i, k=k, f=f: e.tensor_copy(f[:, 0:448], pp[2 * k][:, 0:448]))
            once("vector", f"kf{k}", 1, [(f"kt{k}", None, 7)],
                 lambda e, i, k=k, f=f: e.tensor_copy(f[:, 448:784], pp[2 * k + 1][:, 0:336]))
        once("vector", "kpad", 1, [("kf0", None, 2), ("pid", None, 1)], lambda e, i: e.tensor_scalar(
            keyf[32:64, 781:782], pid[32:64, :], float(PAD_ROW), None, ALU.add))
        once("vector", "kpad", 1, [("kf0", None, 2), ("pid", None, 1)], lambda e, i: e.tensor_scalar(
            keyf[64:128, 781:782], pid[64:128, :], float(PAD_ROW), None, ALU.add))
        once("vector", "keyi", 1, [("kpad", None, 2)], lambda e, i: e.tensor_copy(keyi[:, :], keyf[:, :]))
        once("vector", "kvi", 1, [("kf1", None, 2)], lambda e, i: e.tensor_copy(kvi[:, :], kvf[:, :]))

        once("tensor", "wot", 1, [("wl", None, 20), ("id", None, 1)],
             lambda e, i: e.transpose(pp[4][:, 0:128], woS[:, :], ident[:, :]))
        once("vector", "wot2", 1, [("wot", None, 1)], lambda e, i: e.tensor_copy(woT[:, :], pp[4][:, 0:128]))
        for s in range(2):
            once("vector", "stb", 1, [("wl", None, 20)],
                 lambda e, i, s=s: e.tensor_copy(stq[:, s, :, C:QW], bb[:, :, :]))
        body = [
            ("tensor", "xt", 1, [("xl", None, 2), ("id", None, 1), ("xtc", -2)],
             lambda e, b: e.transpose(pp[5 + b % 2][:, 0:128], xs[:, b, :], ident[:, :])),
            ("vector", "xtc", 1, [("xt", 0)],
             lambda e, b: e.tensor_copy(xT[:, b * 128:(b + 1) * 128], pp[5 + b % 2][:, 0:128])),
        ]
        loop(NB, body, False)
        once("tensor", "pfree", 1, [("kf0", None, 2), ("kf1", None, 2), ("wot2", None, 1), ("xtc", None, NB)],
             lambda e, i: e.transpose(pp[7][:, 0:128], ident[:, :], ident[:, :]))

        def project(e, b, col, psum, width):
            k, c = divmod(col, 640)
            return e.matmul(psum[:, 0:width], xT[:, b * 128:(b + 1) * 128],
                            W[:, k, :, :].rearrange("p r c -> p (r c)")[:, c:c + width], start=True, stop=True)

        body = []
        cuts = ((0, 512), (512, 128), (640, 512), (1152, 128), (1280, 512), (1792, 128))
        for n, (col, width) in enumerate(cuts):
            who = ("vector", "scalar")[n % 2]
            wide = width == 512
            bank = (0, 4, 1, 5, 2, 6)[n]
            if width == 512:
                bank = n // 2
            else:
                bank = 4 + n // 2
            body.append(("tensor", f"pj{n}", 1, [("pfree", None, 1), (f"pc{n}", -1)],
                         lambda e, b, col=col, width=width, bank=bank: project(e, b, col, pp[bank], width)))
            r0, r1 = ((0, 4), (4, 5))[n % 2]

            def put(e, b, n=n, bank=bank, r0=r0, r1=r1, width=width, who=who):
                s = pp[bank][:, 0:width].rearrange("p (r c) -> p r c", c=C)
                k = n // 2
                d = stq[:, b % 2, r0:r1, 0:C] if k == 0 else stg[:, b % 2, r0:r1, (k - 1) * C:k * C]
                if who == "vector":
                    if k == 0:
                        return e.tensor_scalar(d, s, 0.25, None, ALU.mult)
                    return e.tensor_copy(d, s)
                return e.activation(d, s, ACT.Copy, scale=0.25 if k == 0 else 1.0)

            body.append((("vector", "scalar")[n % 2], f"pc{n}", 1, [(f"pj{n}", 0), ("tabq" if n < 2 else "tabk", -2)], put))
        body.append(("sync", "tabq", (16, 2), [("pc0", 0), ("pc1", 0), ("stb", None, 2)], lambda e, b: e.dma_start(
            QT[b * 640:(b + 1) * 640, :].rearrange("(p r) c -> p (r c)", r=R),
            stq[:, b % 2, :, :].rearrange("p r c -> p (r c)"))))
        body.append(("sync", "tabk", (16, 2), [("pc2", 0), ("pc3", 0), ("pc4", 0), ("pc5", 0)], lambda e, b: e.dma_start(
            KV[b * 640:(b + 1) * 640, :].rearrange("(p r) c -> p (r c)", r=R),
            stg[:, b % 2, :, :].rearrange("p r c -> p (r c)"))))
        loop(NB, body, False)

        general(nc, ctx, q, sb, pp, locals())
        finish(nc, ctx, q, sb, pp, locals())

        block = ctx.enter_context(nc.Block())

        @block.sync
        def _(e):
            q.emit("sync", e)
            q.steps["tabq"].wait_all(e, NB)
            q.steps["tabk"].wait_all(e, NB)
            q.steps["mx0"].wait(e, 1)
            q.steps["acc0"].wait(e, 1)
            q.steps["gsm"].wait(e, NT)
            q.steps["gsa"].wait(e, NT)
            q.steps["outd"].wait(e, 2)

        @block.scalar
        def _(e):
            q.emit("scalar", e)

        @block.vector
        def _(e):
            q.emit("vector", e)

        @block.gpsimd
        def _(e):
            q.emit("gpsimd", e)

        @block.tensor
        def _(e):
            q.emit("tensor", e)


def general(nc, ctx, q, sb, pp, v):
    once, loop = q.once, q.loop
    KV, QT, MX, ACC = v["KV"], v["QT"], v["MX"], v["ACC"]
    keyf, keyi, kvi, ident, tri, pid, aggT = (v[k] for k in ("keyf", "keyi", "kvi", "ident", "tri", "pid", "aggT"))
    fillm = sb("fillm", [128, H])
    filla = sb("filla", [128, AW])
    kc = sb("g_kc", [128, 1])
    ki = sb("g_ki", [128, 1], U32)
    vi = sb("g_vi", [128, 1], U32)
    gkv = sb("g_kv", [128, 2 * C])
    gq = sb("g_q", [128, QW])
    gm = sb("g_m", [128, H])
    ga = sb("g_a", [128, AW])
    prod = sb("g_prod", [128, C])
    lg = sb("g_lg", [128, H])
    L = sb("g_L", [128, NT * H])
    ne = sb("g_ne", [128, 128])
    eq = sb("g_eq", [128, 128])
    tmp = sb("g_tmp", [128, 128])
    dup = sb("g_dup", [128, 1])
    dfar = sb("g_dfar", [128, 1])
    wf = sb("g_wf", [128, 1])
    wi = sb("g_wi", [128, 1], U32)
    widx = sb("g_widx", [128, NT], U32)
    X = sb("g_X", [128, H, 128])
    mx = sb("g_mx", [128, H])
    ex = sb("g_ex", [128, H])
    EV = sb("g_EV", [128, AW])
    up = sb("g_up", [128, AW])
    KR, LB0, LB1, TT = pp[0][:, 0:128], pp[1], pp[2], pp[3][:, 0:AW]
    at = bass.ds

    def gather(buf, tab, idx):
        return lambda e, i: e.indirect_dma_start(buf[:, :], None, tab, bass.IndirectOffsetOnAxis(idx[:, 0:1], 0))

    def scatter(buf, tab, idx):
        return lambda e, i: e.indirect_dma_start(tab, bass.IndirectOffsetOnAxis(idx[:, 0:1], 0), buf[:, :], None)

    def row_of(col):
        return lambda e, i: e.matmul(KR, col[:, 0:1].broadcast_to([128, 128]), ident[:, :], start=True, stop=True)

    def spread(e, i):
        for h in range(H):
            last = e.matmul((LB0, LB1)[h // 4][:, (h % 4) * 128:(h % 4 + 1) * 128],
                            lg[:, h:h + 1].broadcast_to([128, 128]), ident[:, :], start=True, stop=True)
        return last

    once("vector", "fm", 1, [], lambda e, i: e.memset(fillm[:, :], NEG))
    once("vector", "fa", 1, [], lambda e, i: e.memset(filla[:, :], 0.0))
    once("sync", "mx0", 16, [("fm", None, 1)], lambda e, i: e.dma_start(
        MX.rearrange("(p r) c -> p r c", p=128), fillm[:, None, :].broadcast_to([128, ROWS // 128, H])))
    once("sync", "acc0", 16, [("fa", None, 1)], lambda e, i: e.dma_start(
        ACC.rearrange("(p r) c -> p r c", p=128), filla[:, None, :].broadcast_to([128, ROWS // 128, AW])))
    once("vector", "dfar", 1, [("pid", None, 1)], lambda e, i: e.tensor_scalar(
        dfar[:, :], pid[:, :], float(DUP_ROW), None, ALU.add))

    loop(NT, [
        ("vector", "akc", 1, [("kpad", None, 2), ("adup", -1), ("awf", -1), ("akr", -1)],
         lambda e, i: e.tensor_copy(kc[:, :], keyf[:, at(i, 1)])),
        ("vector", "aki", 1, [("keyi", None, 1), ("agq", -1), ("agm", -1)],
         lambda e, i: e.tensor_copy(ki[:, :], keyi[:, at(i, 1)])),
        ("vector", "avi", 1, [("kvi", None, 1), ("agk", -1)],
         lambda e, i: e.tensor_copy(vi[:, :], kvi[:, at(i, 1)])),
        ("gpsimd", "agk", 16, [("avi", 0), ("tabk", None, NB), ("aprod", -1)], gather(gkv, KV, vi)),
        ("gpsimd", "agq", 16, [("aki", 0), ("tabq", None, NB), ("alg", -1)], gather(gq, QT, ki)),
        ("gpsimd", "agm", 16, [("aki", 0), ("mx0", None, 1), ("gsm", -1), ("amx2", -1)], gather(gm, MX, ki)),
        ("tensor", "akr", 1, [("akc", 0), ("id", None, 1), ("aeq", -1), ("pc0", None, NB)], row_of(kc)),
        ("vector", "ane", 1, [("akr", 0), ("akc", 0), ("aX0", -1), ("aX1", -1)], lambda e, i: e.tensor_scalar(
            ne[:, :], KR, kc[:, 0:1], FAR, ALU.not_equal, ALU.mult)),
        ("vector", "aeq", 1, [("akr", 0), ("akc", 0), ("adup", -1)], lambda e, i: e.tensor_scalar(
            eq[:, :], KR, kc[:, 0:1], None, ALU.is_equal)),
        ("vector", "atmp", 1, [("aeq", 0), ("tri", None, 1), ("adup", -1)], lambda e, i: e.tensor_tensor(
            tmp[:, :], eq[:, :], tri[:, :], ALU.mult)),
        ("vector", "adup", 1, [("atmp", 0), ("awf", -1)], lambda e, i: e.tensor_reduce(
            dup[:, :], tmp[:, :], AX.X, ALU.add)),
        ("vector", "adup1", 1, [("adup", 0)], lambda e, i: e.tensor_scalar(
            dup[:, :], dup[:, :], 0.0, None, ALU.is_gt)),
        ("vector", "awf0", 1, [("akc", 0), ("dfar", None, 1), ("awi", -1)], lambda e, i: e.tensor_tensor(
            wf[:, :], dfar[:, :], kc[:, :], ALU.subtract)),
        ("vector", "awf1", 1, [("awf0", 0), ("adup1", 0)], lambda e, i: e.tensor_tensor(
            wf[:, :], wf[:, :], dup[:, :], ALU.mult)),
        ("vector", "awf", 1, [("awf1", 0)], lambda e, i: e.tensor_tensor(
            wf[:, :], wf[:, :], kc[:, :], ALU.add)),
        ("vector", "awi", 1, [("awf", 0), ("gsm", -1)], lambda e, i: e.tensor_copy(wi[:, :], wf[:, :])),
        ("vector", "awx", 1, [("awf", 0)], lambda e, i: e.tensor_copy(widx[:, at(i, 1)], wf[:, :])),
        ("vector", "aprod", 1, [("agk", 0), ("agq", 0), ("alg0", -1)], lambda e, i: e.tensor_tensor(
            prod[:, :], gkv[:, 0:C], gq[:, 0:C], ALU.mult)),
        ("vector", "alg0", 1, [("aprod", 0), ("abc", -1)], lambda e, i: e.tensor_reduce(
            lg[:, :], prod[:, :].rearrange("p (h d) -> p h d", d=D), AX.X, ALU.add)),
        ("vector", "alg", 1, [("alg0", 0), ("agq", 0)], lambda e, i: e.tensor_tensor(
            lg[:, :], lg[:, :], gq[:, C:QW], ALU.add)),
        ("vector", "aL", 1, [("alg", 0)], lambda e, i: e.tensor_copy(L[:, at(i * H, H)], lg[:, :])),
        ("tensor", "abc", 1, [("alg", 0), ("aX0", -1), ("aX1", -1), ("pc2", None, NB), ("pc4", None, NB)], spread),
        ("vector", "aX0", 1, [("abc", 0), ("ane", 0), ("amx", -1)], lambda e, i: e.tensor_tensor(
            X[:, 0:4, :], LB0[:, :].rearrange("p (h j) -> p h j", h=4),
            ne[:, None, :].broadcast_to([128, 4, 128]), ALU.add)),
        ("vector", "aX1", 1, [("abc", 0), ("ane", 0), ("amx", -1)], lambda e, i: e.tensor_tensor(
            X[:, 4:8, :], LB1[:, :].rearrange("p (h j) -> p h j", h=4),
            ne[:, None, :].broadcast_to([128, 4, 128]), ALU.add)),
        ("vector", "amx", 1, [("aX0", 0), ("aX1", 0), ("gsm", -1)], lambda e, i: e.tensor_reduce(
            mx[:, :], X[:, :, :], AX.X, ALU.max)),
        ("vector", "amx2", 1, [("amx", 0), ("agm", 0)], lambda e, i: e.tensor_tensor(
            mx[:, :], mx[:, :], gm[:, :], ALU.max)),
        ("gpsimd", "gsm", 16, [("amx2", 0), ("awi", 0), ("agm", 0)], scatter(mx, MX, wi)),
    ], True)

    loop(NT, [
        ("vector", "bkc", 1, [("beq", -1), ("bkr", -1), ("gsm", None, NT), ("akr", None, NT), ("abc", None, NT)],
         lambda e, i: e.tensor_copy(kc[:, :], keyf[:, at(i, 1)])),
        ("vector", "bki", 1, [("bgm", -1), ("bga", -1)],
         lambda e, i: e.tensor_copy(ki[:, :], keyi[:, at(i, 1)])),
        ("vector", "bvi", 1, [("bgk", -1)], lambda e, i: e.tensor_copy(vi[:, :], kvi[:, at(i, 1)])),
        ("vector", "bwi", 1, [("gsa", -1), ("awx", None, NT)],
         lambda e, i: e.tensor_copy(wi[:, :], widx[:, at(i, 1)])),
        ("gpsimd", "bgk", 16, [("bvi", 0), ("bev", -1)], gather(gkv, KV, vi)),
        ("gpsimd", "bgm", 16, [("bki", 0), ("bsub", -1)], gather(gm, MX, ki)),
        ("gpsimd", "bga", 16, [("bki", 0), ("acc0", None, 1), ("gsa", -1), ("bup", -1)], gather(ga, ACC, ki)),
        ("tensor", "bkr", 1, [("bkc", 0), ("beq", -1)], row_of(kc)),
        ("vector", "beq", 1, [("bkr", 0), ("bkc", 0), ("btt", -1)], lambda e, i: e.tensor_scalar(
            eq[:, :], KR, kc[:, 0:1], None, ALU.is_equal)),
        ("vector", "bsub", 1, [("bgm", 0), ("bexp", -1), ("aL", None, NT)], lambda e, i: e.tensor_tensor(
            ex[:, :], L[:, at(i * H, H)], gm[:, :], ALU.subtract)),
        ("scalar", "bexp", 1, [("bsub", 0), ("btt", -1)], lambda e, i: e.activation(
            EV[:, C:AW], ex[:, :], ACT.Exp)),
        ("vector", "bev", 1, [("bexp", 0), ("bgk", 0), ("btt", -1)], lambda e, i: e.tensor_tensor(
            EV[:, 0:C].rearrange("p (h d) -> p h d", d=D), gkv[:, C:2 * C].rearrange("p (h d) -> p h d", d=D),
            EV[:, C:AW, None].broadcast_to([128, H, D]), ALU.mult)),
        ("tensor", "btt", 1, [("bev", 0), ("beq", 0), ("bup", -1), ("pc5", None, NB)], lambda e, i: e.matmul(
            TT, eq[:, :], EV[:, :], start=True, stop=True)),
        ("vector", "bup", 1, [("btt", 0), ("bga", 0), ("gsa", -1)], lambda e, i: e.tensor_tensor(
            up[:, :], ga[:, :], TT, ALU.add)),
        ("gpsimd", "gsa", 16, [("bup", 0), ("bwi", 0), ("bga", 0)], scatter(up, ACC, wi)),
    ], True)

    ca = sb("c_a", [128, R, AW])
    cs = sb("c_s", [128, R, H])
    cg = sb("c_g", [128, C])
    loop(NB, [
        ("sync", "cld", 16, [("gsa", None, NT), ("cmul", -1)], lambda e, b: e.dma_start(
            ca[:, :, :].rearrange("p r c -> p (r c)"),
            ACC[b * 640:(b + 1) * 640, :].rearrange("(p r) c -> p (r c)", r=R))),
        ("vector", "ceps", 1, [("cld", 0), ("cmul", -1)], lambda e, b: e.tensor_scalar(
            cs[:, :, :], ca[:, :, C:AW], 1e-12, None, ALU.add)),
        ("vector", "crec", 1, [("ceps", 0)], lambda e, b: e.reciprocal(cs[:, :, :], cs[:, :, :])),
    ] + [
        ("vector", f"cm{r}", 1, [("crec", 0)], lambda e, b, r=r: e.tensor_tensor(
            ca[:, r, 0:C].rearrange("p (h d) -> p h d", d=D), ca[:, r, 0:C].rearrange("p (h d) -> p h d", d=D),
            cs[:, r, :, None].broadcast_to([128, H, D]), ALU.mult)) for r in range(R)
    ] + [
        ("vector", "cmul", 1, [(f"cm{r}", 0) for r in range(R)] + [("ctr", -1)], lambda e, b: e.tensor_reduce(
            cg[:, :], ca[:, :, 0:C].rearrange("p r c -> p c r"), AX.X, ALU.add)),
        ("tensor", "ctr", 1, [("cmul", 0), ("agg", -1)], lambda e, b: e.transpose(
            pp[4][:, 0:128], cg[:, :], ident[:, :])),
        ("vector", "agg", 1, [("ctr", 0)], lambda e, b: e.tensor_copy(
            aggT[:, b * 128:(b + 1) * 128], pp[4][:, 0:128])),
    ], False)


def finish(nc, ctx, q, sb, pp, v):
    loop = q.loop
    xs, aggT, woT, bob, gab, beb, out = (v[k] for k in ("xs", "aggT", "woT", "bob", "gab", "beb", "out"))
    hb = sb("f_h", [128, 2, C])
    st = sb("f_st", [128, 2, 6])
    mv = sb("f_mv", [128, 2, 2])
    sd = sb("f_sd", [128, 2])
    res = v["xT"][:, :].rearrange("p (b c) -> p b c", c=C)
    epst = sb("f_eps", [128, 1])
    q.once("vector", "feps", 1, [], lambda e, i: e.memset(epst[:, :], EPS))

    def stats(p, src, before):
        return [
            ("vector", f"{p}bs", 1, before, lambda e, b: e.bn_stats(st[:, b % 2, :], src(b))),
            ("vector", f"{p}ba", 1, [(f"{p}bs", 0)], lambda e, b: e.bn_aggr(mv[:, b % 2, :], st[:, b % 2, :])),
            ("scalar", f"{p}sq", 1, [(f"{p}ba", 0), ("feps", None, 1)], lambda e, b: e.activation(
                sd[:, b % 2:b % 2 + 1], mv[:, b % 2, 1:2], ACT.Sqrt, bias=epst[:, 0:1])),
            ("vector", f"{p}rc", 1, [(f"{p}sq", 0)], lambda e, b: e.reciprocal(
                sd[:, b % 2:b % 2 + 1], sd[:, b % 2:b % 2 + 1])),
            ("vector", f"{p}nm", 1, [(f"{p}rc", 0)], lambda e, b: e.tensor_scalar(
                src(b), src(b), mv[:, b % 2, 0:1], sd[:, b % 2:b % 2 + 1], ALU.subtract, ALU.mult)),
        ]

    h = lambda b: hb[:, b % 2, :]
    body = [
        ("tensor", "fo", 1, [("agg", None, NB), ("fh0", -1)], lambda e, b: e.matmul(
            pp[6][:, 0:128], aggT[:, b * 128:(b + 1) * 128], woT[:, :], start=True, stop=True)),
        ("vector", "fh0", 1, [("fo", 0), ("fcp", -1)], lambda e, b: e.tensor_tensor(h(b), pp[6][:, 0:128], bob[:, :], ALU.add)),
        ("vector", "fh1", 1, [("fh0", 0)], lambda e, b: e.tensor_tensor(h(b), h(b), xs[:, b, :], ALU.add)),
    ] + stats("f", h, [("fh1", 0)]) + [
        ("vector", "fg", 1, [("fnm", 0)], lambda e, b: e.tensor_tensor(h(b), h(b), gab[:, :], ALU.mult)),
        ("vector", "fb", 1, [("fg", 0)], lambda e, b: e.tensor_tensor(h(b), h(b), beb[:, :], ALU.add)),
        ("vector", "fx", 1, [("fb", 0)], lambda e, b: e.tensor_tensor(h(b), h(b), xs[:, b, :], ALU.add)),
    ] + stats("g", h, [("fx", 0)]) + [
        ("vector", "fcp", 1, [("gnm", 0), ("pj5", None, NB)], lambda e, b: e.tensor_copy(res[:, b, :], h(b))),
    ]
    loop(NB, body, False)
    q.once("sync", "outd", 16, [("fcp", None, NB)], lambda e, i: e.dma_start(
        out[0:3072, :].rearrange("(b p) c -> p b c", p=128), res[:, 0:24, :]))
    q.once("sync", "outd", 16, [("fcp", None, NB)], lambda e, i: e.dma_start(out[3072:N, :], res[0:53, 24, :]))


_INS = ["x", "src", "dst", "edge_type_5", "L0_gnn_W_Q", "L0_gnn_W_K", "L0_gnn_W_V", "L0_gnn_attn_bias",
        "L0_gnn_out_proj_w", "L0_gnn_out_proj_b", "L0_gnn_ln_gamma", "L0_gnn_ln_beta"]


def kernel(**inputs):
    import numpy as np
    import concourse.bacc as bacc
    from concourse.bass_utils import run_bass_kernel_spmd

    nc = bacc.Bacc("TRN2", target_bir_lowering=False, num_devices=1)
    arrays, args = {}, []
    for name in _INS:
        a = np.ascontiguousarray(inputs[name])
        arrays["in_" + name] = a
        args.append(nc.dram_tensor("in_" + name, a.shape, mybir.dt.from_np(a.dtype), kind="ExternalInput").ap())
    args.append(nc.dram_tensor("out_0", (N, C), F32, kind="ExternalOutput").ap())
    build(nc, *args)
    r = run_bass_kernel_spmd(nc, [arrays], core_ids=[0])
    return r.results[0]["out_0"]
```

```python
import concourse.bass as bass
from concourse import mybir
from contextlib import ExitStack

N = 3125
E = 100000
R = 5
H = 8
D = 16
C = 128
NB = 25
NQ = 196
HQ = 98
NT = 4 * NQ
KEYS = N * R
DUP_ROW = KEYS + 128
ROWS = 16128
QW = C + H
AW = C + H
NEG = -1.0e9
FAR = -1.0e30
EPS = 1e-5
SPAN = 24
SLOTS = 64
LC = H + 1
LAG = 22
KR = 26
OR = 24
PF = 3
SEEK = 500

F32 = mybir.dt.float32
BF16 = mybir.dt.bfloat16
I32 = mybir.dt.int32
U32 = mybir.dt.uint32
ALU = mybir.AluOpType
ACT = mybir.ActivationFunctionType
AX = mybir.AxisListType


def first_quad(b):
    return max(8 * b - 2, 0)


def last_quad(b):
    return min(8 * b + 9, NQ - 1)


def last_block(q):
    return min((16 * q + 58) // 128, NB - 1)


class Own:

    def __init__(self, sems, inc, per):
        self.sems = sems
        self.inc = inc
        self.per = per

    def wait(self, eng, turn):
        n = len(self.sems)
        if n == 1:
            eng.wait_ge(self.sems[0], (turn + 1) * (self.inc * self.per))
        else:
            eng.wait_ge(self.sems[turn % n], (turn // n + 1) * self.inc * self.per)

    def wait_all(self, eng, times):
        for t in range(max(times - len(self.sems), 0), times):
            self.wait(eng, t)

    def end(self, ins, i):
        sem = self.sems[0] if len(self.sems) == 1 else self.sems[i % len(self.sems)]
        for one in ins if isinstance(ins, list) else [ins]:
            one.then_inc(sem, self.inc)


class Counted:

    def __init__(self, sem, per):
        self.sem = sem
        self.per = per
        self.values = []

    def wait(self, eng, turn):
        eng.wait_ge(self.sem, self.values[turn])

    def wait_all(self, eng, times):
        self.wait(eng, times - 1)

    def end(self, ins, i):
        for one in ins if isinstance(ins, list) else [ins]:
            one.then_inc(self.sem, 1)


class Queues:

    def __init__(self, nc, ctx, parent=None):
        self.nc = nc
        self.ctx = ctx
        self.parent = parent
        self.steps = dict(parent.steps) if parent else {}
        names = ("scalar", "vector", "gpsimd", "tensor")
        self.tick = parent.tick if parent else ctx.enter_context(nc.semaphore("tick"))
        self.counts = parent.counts if parent else {k: ctx.enter_context(nc.semaphore("n_" + k)) for k in names}
        self.count = {}
        self.lists = {"sync": [], "scalar": [], "vector": [], "gpsimd": [], "tensor": []}

    def step(self, eng, name, inc, rolled):
        if name in self.steps:
            return
        inc, n, per = (*inc, 1)[:3] if isinstance(inc, tuple) else (inc, 1, 1)
        if inc == 1 and not rolled:
            self.steps[name] = Counted(self.counts[eng], per)
        else:
            self.steps[name] = Own([self.ctx.enter_context(self.nc.semaphore(f"s_{name}_{k}")) for k in range(n)],
                                   inc, per)

    def loop(self, count, body, rolled):
        for eng, name, inc, _, _ in body:
            self.step(eng, name, inc, rolled)
        for key in self.lists:
            mine = [b for b in body if b[0] == key]
            if not mine:
                continue
            if rolled:
                self.lists[key].append((None, mine, count))
            else:
                for i in range(count):
                    for _, name, inc, after, emit in mine:
                        fixed = [a if len(a) == 3 else (a[0], i + a[1]) for a in after]
                        self.lists[key].append((i, name, fixed, lambda e, i=i, emit=emit: emit(e, i)))

    def once(self, eng, name, inc, after, emit):
        self.step(eng, name, inc, False)
        self.lists[eng].append((-1, name, after, lambda e: emit(e, 0)))

    def at(self, eng, name, inc, turn, after, emit):
        self.step(eng, name, inc, False)
        self.lists[eng].append((turn, name, after, emit))

    def number(self):
        self.count = dict(self.parent.count) if self.parent else dict.fromkeys(self.lists, 0)
        for key, entries in self.lists.items():
            for turn, name, *_ in entries:
                if turn is not None and isinstance(self.steps[name], Counted):
                    one = self.steps[name]
                    self.count[key] += one.per
                    assert turn in (-1, len(one.values)), (name, turn, len(one.values))
                    one.values.append(self.count[key])

    def turn(self, eng, mine, i, key):
        for _, name, _, after, emit in mine:
            for a in after:
                if len(a) == 3:
                    self.steps[a[0]].wait_all(eng, a[2])
                elif a[1] == 0 or not isinstance(i, int) or i + a[1] >= 0:
                    self.steps[a[0]].wait(eng, i + a[1])
            if key == "gpsimd":
                eng.sem_inc(self.tick, 1)
            self.steps[name].end(emit(eng, i), i)

    def emit(self, key, eng):
        for entry in self.lists[key]:
            if entry[0] is None:
                _, mine, count = entry
                self.turn(eng, mine, 0, key)
                with eng.Fori(1, count) as i:
                    self.turn(eng, mine, i, key)
                continue
            turn, name, after, emit = entry
            for a in after:
                if len(a) == 3:
                    self.steps[a[0]].wait_all(eng, a[2])
                elif a[1] >= 0:
                    self.steps[a[0]].wait(eng, a[1])
            self.steps[name].end(emit(eng), max(turn, 0))


class Region:

    def __init__(self, ap):
        self.ap = ap
        self.off = 0

    def take(self, shape, dt=F32, parts=128):
        n = 1
        for k in shape:
            n *= k
        words = n if dt not in (BF16,) else (n + 1) // 2
        a = self.ap[0:parts, self.off:self.off + words]
        self.off += words
        if dt != F32:
            a = a.bitcast(dt)
        names = "abcde"[:len(shape)]
        if len(shape) > 1:
            a = a.rearrange(f"p ({' '.join(names)}) -> p {' '.join(names)}",
                            **{m: k for m, k in zip(names, shape)})
        return a


def build(nc, x, src, dst, typ, wq, wk, wv, bias, wo, bo, gamma, beta, out):
    ctx = ExitStack()
    with ctx:
        def sb(name, shape, dt=F32):
            return ctx.enter_context(nc.sbuf_tensor(name, shape, dt))

        def ps(name, shape, dt=F32):
            return ctx.enter_context(nc.psum_tensor(name, shape, dt))

        KV = nc.dram_tensor("KVtab", [NB * 640, 2 * C], F32).ap()
        QT = nc.dram_tensor("Qtab", [NB * 640, QW], F32).ap()
        MX = nc.dram_tensor("MXtab", [ROWS, H], F32).ap()
        ACC = nc.dram_tensor("ACCtab", [ROWS, AW], F32).ap()
        CT = nc.dram_tensor("Ctab", [NB * 640, 48], BF16).ap()
        LB = [nc.dram_tensor(f"Ltab{b}", [(last_quad(b) - first_quad(b) + 1) * 512, LC], F32).ap() for b in range(NB)]

        ring = sb("ring", [128, KR * 4 * 2 * C])
        pool = sb("pool", [128, 11776])
        xs = sb("xs", [128, NB, C])
        aggT = sb("aggT", [128, NB * 128 + 32])
        hb = sb("hb", [128, 5, C])
        keyf = sb("keyf", [128, NT])
        kvi = sb("kvi", [128, NT], U32)
        relk = sb("relk", [128, NT], BF16)
        reln = sb("reln", [128, NT], BF16)
        woT = sb("woT", [128, C])
        bb = sb("bb", [128, R, H])
        bob = sb("bob", [128, C])
        gab = sb("gab", [128, C])
        beb = sb("beb", [128, C])
        ident = sb("ident", [128, 128])
        identb = sb("identb", [128, 128], BF16)
        pid = sb("pid", [128, 1])
        nk = sb("nk", [128, R, NB])
        io32 = sb("io32", [128, 32], BF16)
        strel = sb("strel", [128, NB], U32)
        n0i = sb("n0i", [1, NQ], I32)
        kbi = sb("kbi", [1, NQ], I32)
        flag = sb("flag", [1, 1], I32)
        pp = [ps(f"pp{i}", [128, 512]) for i in range(8)]

        early = Region(pool[:, :])
        xT = early.take([NB * 128])
        W = early.take([3, R, C])
        stg = early.take([2, R, 2 * C])
        stq = early.take([2, R, QW])
        assert early.off <= 11776 + 0
        temp = Region(ring[:, :])
        natd = temp.take([2, 577], I32, HQ)
        nats = temp.take([2, 512], I32, HQ)
        natt = temp.take([2, 512], I32, HQ)
        fd = temp.take([2, 577], F32, HQ)
        fs = temp.take([2, 512], F32, HQ)
        ft = temp.take([2, 512], F32, HQ)
        junk = natd.bitcast(F32)[:, :, 0:576]
        far5 = temp.take([2, 2], I32, 100)
        far5f = temp.take([2, 2], F32, 100)
        cmp1 = temp.take([NB, 200])
        woS = temp.take([C])
        rows = temp.take([NB, SEEK], I32)
        rowsf = rows.bitcast(F32)
        nf = temp.take([NB])
        cnt = temp.take([NB])
        qi = temp.take([NB], U32)
        cnt2 = temp.take([NB])
        stf = temp.take([NB])
        n0f = temp.take([NQ])
        t4 = temp.take([NQ, 4])
        viol = temp.take([4], F32, HQ)
        v196 = temp.take([NQ])
        lim6 = temp.take([NQ])
        v25 = temp.take([2, NB])
        tot = temp.take([8])
        ones = temp.take([1])
        base = temp.take([NB])

        q = Queues(nc, ctx)
        once, loop = q.once, q.loop

        once("gpsimd", "id0", 1, [], lambda e, i: e.memset(ident[:, :], 0.0))
        once("gpsimd", "id", 1, [("id0", None, 1)], lambda e, i: e.affine_select(
            out=ident[:, :], in_=ident[:, :], compare_op=ALU.not_equal, fill=1.0, base=0,
            pattern=[[-1, 128]], channel_multiplier=1))
        once("gpsimd", "pid", 1, [], lambda e, i: e.iota(
            pid[:, :], [[0, 1]], base=0, channel_multiplier=1, allow_small_or_imprecise_dtypes=True))
        once("gpsimd", "nf", 1, [], lambda e, i: e.iota(
            nf[:, :], [[128, NB]], base=0, channel_multiplier=1, allow_small_or_imprecise_dtypes=True))
        once("gpsimd", "nk", 1, [], lambda e, i: e.iota(
            nk[:, :, :], [[1, R], [640, NB]], base=0, channel_multiplier=5, allow_small_or_imprecise_dtypes=True))
        once("gpsimd", "io32", 1, [], lambda e, i: e.iota(
            io32[:, :], [[1, 32]], base=0, channel_multiplier=0, allow_small_or_imprecise_dtypes=True))
        once("gpsimd", "base", 1, [], lambda e, i: e.iota(
            base[:, :], [[4096, NB]], base=0, channel_multiplier=0, allow_small_or_imprecise_dtypes=True))
        once("gpsimd", "ones", 1, [], lambda e, i: e.memset(ones[:, :], 1.0))
        edge = 0
        for b in range(NB):
            end = edge
            while end < NQ and last_block(end) == b:
                end += 1
            if end > edge:
                once("gpsimd", "lim6", 1, [], lambda e, i, a=edge, z=end, b=b: e.memset(
                    lim6[:, a:z], float(128 * (b + 1) - 26)))
            edge = end
        once("vector", "nz", 1, [], lambda e, i: e.memset(natd[:, :, :], N))
        once("vector", "nz", 1, [], lambda e, i: e.memset(nats[:, 1, :], 0))
        once("vector", "nz", 1, [], lambda e, i: e.memset(natt[:, 1, :], 0))
        once("vector", "xz", 1, [], lambda e, i: e.memset(xs[:, 24, :], 0.0))

        def window(c, n):
            v = dst[0:n * 512].rearrange("(r c) -> r c", c=512)
            return v

        once("sync", "nat", 16, [("nz", None, 3)], lambda e, i: e.dma_start(
            natd[0:98, 0, 0:512], dst[0:HQ * 512].rearrange("(r c) -> r c", c=512)))
        once("sync", "nat", 16, [("nz", None, 3)], lambda e, i: e.dma_start(
            natd[0:98, 0, 512:577], dst[512:512 + HQ * 512].rearrange("(r c) -> r c", c=512)[:, 0:65]))
        once("sync", "nat", 16, [("nz", None, 3)], lambda e, i: e.dma_start(
            natd[0:97, 1, 0:512], dst[HQ * 512:195 * 512].rearrange("(r c) -> r c", c=512)))
        once("sync", "nat", 16, [("nz", None, 3)], lambda e, i: e.dma_start(
            natd[0:96, 1, 512:577], dst[99 * 512:195 * 512].rearrange("(r c) -> r c", c=512)[:, 0:65]))
        once("sync", "nat", 16, [("nz", None, 3)], lambda e, i: e.dma_start(
            natd[96:97, 1, 512:577], dst[195 * 512:195 * 512 + 65].rearrange("(r c) -> r c", r=1)))
        once("sync", "nat", 16, [("nz", None, 3)], lambda e, i: e.dma_start(
            natd[97:98, 1, 0:160], dst[195 * 512:E].rearrange("(r c) -> r c", r=1)))
        for t, a in ((nats, src), (natt, typ)):
            once("sync", "nat", 16, [], lambda e, i, t=t, a=a: e.dma_start(
                t[0:98, 0, :], a[0:HQ * 512].rearrange("(r c) -> r c", c=512)))
            once("sync", "nat", 16, [("nz", None, 3)], lambda e, i, t=t, a=a: e.dma_start(
                t[0:97, 1, :], a[HQ * 512:195 * 512].rearrange("(r c) -> r c", c=512)))
            once("sync", "nat", 16, [("nz", None, 3)], lambda e, i, t=t, a=a: e.dma_start(
                t[97:98, 1, 0:160], a[195 * 512:E].rearrange("(r c) -> r c", r=1)))
        for c in range(2):
            once("sync", "nat", 16, [], lambda e, i, c=c: e.dma_start(
                far5[:, c, :], dst[c * 50000:(c + 1) * 50000].rearrange("(r c) -> r c", c=SEEK)[:, 0:2]))
        NNAT = 14
        once("scalar", "xl", 16, [], lambda e, i: e.dma_start(
            xs[:, 0:24, :], x[0:3072, :].rearrange("(b p) c -> p b c", p=128)))
        once("scalar", "xl", 16, [("xz", None, 1)], lambda e, i: e.dma_start(xs[0:53, 24, :], x[3072:N, :]))
        for k, a in ((1, wk), (2, wv), (0, wq)):
            for r in range(R):
                once("scalar", "wl" if k else "wlq", 16, [], lambda e, i, k=k, a=a, r=r: e.dma_start(
                    W[:, k, r, :].rearrange("p (k d) -> p k d", d=D), a[r].rearrange("k h d -> h k d")))
        once("scalar", "wlo", 16, [], lambda e, i: e.dma_start(woS[:, :], wo))
        once("scalar", "wlo", 16, [], lambda e, i: e.dma_start(
            bb[:, :, :].rearrange("p r h -> p (r h)"),
            bias.rearrange("r h -> (r h)").partition_broadcast(128)))
        for dst_, a in ((bob, bo), (gab, gamma), (beb, beta)):
            once("scalar", "wlo", 16, [], lambda e, i, d=dst_, a=a: e.dma_start(d[:, :], a.partition_broadcast(128)))

        once("vector", "f5", 1, [("nat", None, NNAT)], lambda e, i: e.tensor_copy(far5f[:, :, :], far5[:, :, :]))
        once("vector", "fd", 1, [("nat", None, NNAT)], lambda e, i: e.tensor_copy(fd[:, :, :], natd[:, :, :]))
        once("vector", "idb", 1, [("id", None, 1)], lambda e, i: e.tensor_copy(identb[:, :], ident[:, :]))
        once("tensor", "f5b", 1, [("f5", None, 1), ("id", None, 1)], lambda e, i: e.matmul(
            pp[6][:, 0:100], far5f[:, 0, 0:1].broadcast_to([100, 128]), ident[0:100, 0:100], start=True, stop=True))
        once("tensor", "f5b", 1, [("f5", None, 1)], lambda e, i: e.matmul(
            pp[6][:, 100:200], far5f[:, 1, 0:1].broadcast_to([100, 128]), ident[0:100, 0:100], start=True, stop=True))
        once("vector", "cmp1", 1, [("f5b", None, 2), ("nf", None, 1)], lambda e, i: e.tensor_tensor(
            cmp1[:, :, :], pp[6][:, None, 0:200].broadcast_to([128, NB, 200]),
            nf[:, :, None].broadcast_to([128, NB, 200]), ALU.is_lt))
        once("vector", "cnt", 1, [("cmp1", None, 1)], lambda e, i: e.tensor_reduce(
            cnt[:, :], cmp1[:, :, :], AX.X, ALU.add))
        once("vector", "cnt1", 1, [("cnt", None, 1)], lambda e, i: e.tensor_scalar(
            cnt[:, :], cnt[:, :], -1.0, 0.0, ALU.add, ALU.max))
        once("vector", "qi", 1, [("cnt1", None, 1)], lambda e, i: e.tensor_copy(qi[:, :], cnt[:, :]))
        for b in range(NB):
            once("gpsimd", "rows", (16, 1), [("qi", None, 1)], lambda e, i, b=b: e.indirect_dma_start(
                rows[:, b, :], None, dst.rearrange("(r c) -> r c", c=SEEK),
                bass.IndirectOffsetOnAxis(qi[:, b:b + 1], 0)))
        once("vector", "fs", 1, [("nat", None, NNAT)], lambda e, i: e.tensor_copy(fs[:, :, :], nats[:, :, :]))
        once("vector", "ft", 1, [("nat", None, NNAT)], lambda e, i: e.tensor_copy(ft[:, :, :], natt[:, :, :]))
        once("vector", "fkv", 1, [("fs", None, 1), ("ft", None, 1)], lambda e, i: e.scalar_tensor_tensor(
            fs[:, :, :], fs[:, :, :], 5.0, ft[:, :, :], ALU.mult, ALU.add))
        once("vector", "fk", 1, [("fkv", None, 1), ("fd", None, 1)], lambda e, i: e.scalar_tensor_tensor(
            ft[:, :, :], fd[:, :, 0:512], 5.0, ft[:, :, :], ALU.mult, ALU.add))
        for m, (name, plane, need) in enumerate((("tn", fd, "fd"), ("tv", fs, "fkv"), ("tk", ft, "fk"))):
            for c in range(2):
                for j in range(4):
                    once("tensor", name, 1, [(need, None, 1), ("id", None, 1)],
                         lambda e, i, m=m, c=c, j=j, plane=plane: e.transpose(
                             pp[2 * m + c][:, j * HQ:(j + 1) * HQ], plane[:, c, j:512:4], ident[0:HQ, 0:HQ]))
        for c in range(2):
            once("tensor", "tn0", 1, [("fd", None, 1), ("id", None, 1)], lambda e, i, c=c: e.matmul(
                pp[7][:, c * HQ:(c + 1) * HQ], fd[:, c, 0:1].broadcast_to([HQ, 128]), ident[0:HQ, 0:HQ],
                start=True, stop=True))

        def turned(m, c):
            return pp[2 * m + c][:, 0:4 * HQ].rearrange("p (j r) -> p r j", j=4)

        def place(t, c):
            return t[:, c * 4 * HQ:(c + 1) * 4 * HQ].rearrange("p (r j) -> p r j", j=4)

        once("vector", "n0f", 1, [("tn0", None, 2)], lambda e, i: e.tensor_copy(n0f[:, :], pp[7][:, 0:NQ]))
        once("vector", "n0i", 1, [("n0f", None, 1)], lambda e, i: e.tensor_copy(n0i[:, :], n0f[0:1, :]))
        once("vector", "kbi", 1, [("n0f", None, 1)], lambda e, i: e.tensor_scalar(
            kbi[:, :], n0f[0:1, :], 5.0, None, ALU.mult))
        for c in range(2):
            once("vector", "keyf", 1, [("tk", None, 8)], lambda e, i, c=c: e.tensor_copy(place(keyf, c), turned(2, c)))
            once("vector", "kvi", 1, [("tv", None, 8)], lambda e, i, c=c: e.tensor_copy(place(kvi, c), turned(1, c)))
            once("vector", "reln", 1, [("tn", None, 8), ("n0f", None, 1)], lambda e, i, c=c: e.tensor_tensor(
                place(reln, c), turned(0, c), n0f[:, c * HQ:(c + 1) * HQ, None].broadcast_to([128, HQ, 4]),
                ALU.subtract))
        once("vector", "t4", 1, [("n0f", None, 1), ("keyf", None, 2)], lambda e, i: e.scalar_tensor_tensor(
            t4[:, :, :], n0f[:, :, None].broadcast_to([128, NQ, 4]), -5.0,
            keyf[:, :].rearrange("p (q j) -> p q j", j=4), ALU.mult, ALU.add))
        once("vector", "pad", 1, [("keyf", None, 2)], lambda e, i: e.tensor_scalar(
            cmp1.rearrange("p a b -> p (a b)")[:, 0:NT], keyf[:, :], float(KEYS), -1000.0, ALU.is_ge, ALU.mult))
        once("vector", "relk", 1, [("pad", None, 1), ("t4", None, 1)], lambda e, i: e.tensor_tensor(
            relk[:, :], cmp1.rearrange("p a b -> p (a b)")[:, 0:NT], t4.rearrange("p a b -> p (a b)"), ALU.add))

        once("vector", "v1", 1, [("fd", None, 1)], lambda e, i: e.tensor_tensor(
            junk[:, :, :], fd[:, :, 1:577], fd[:, :, 0:576], ALU.is_lt))
        once("vector", "v1r", 1, [("v1", None, 1)], lambda e, i: e.tensor_reduce(
            viol[:, 0:1], junk[:, :, :], AX.XY, ALU.add))
        once("vector", "v2", 1, [("v1r", None, 1)], lambda e, i: e.tensor_tensor(
            junk[:, :, 0:512], fd[:, :, 64:576], fd[:, :, 0:512], ALU.is_equal))
        once("vector", "v2r", 1, [("v2", None, 1)], lambda e, i: e.tensor_reduce(
            viol[:, 1:2], junk[:, :, 0:512], AX.XY, ALU.add))
        once("vector", "v3", 1, [("fd", None, 1)], lambda e, i: e.tensor_tensor(
            viol[:, 2:4], fd[:, :, 511], fd[:, :, 0], ALU.subtract))
        once("vector", "v3r", 1, [("v3", None, 1)], lambda e, i: e.tensor_scalar(
            viol[:, 2:4], viol[:, 2:4], float(SPAN), None, ALU.is_gt))
        once("tensor", "vt", 1, [("v1r", None, 1), ("v2r", None, 1), ("v3r", None, 1), ("ones", None, 1), ("n0f", None, 1)],
             lambda e, i: e.matmul(pp[7][0:1, 256:260], ones[0:HQ, :], viol[:, :], start=True, stop=True))
        once("vector", "tot", 1, [("vt", None, 1)], lambda e, i: e.tensor_copy(tot[0:1, 0:4], pp[7][0:1, 256:260]))
        once("vector", "tot1", 1, [("tot", None, 1)], lambda e, i: e.tensor_scalar(
            tot[0:1, 1:2], tot[0:1, 1:2], 352.0, None, ALU.not_equal))
        once("vector", "v6", 1, [("n0f", None, 1), ("lim6", None, NB)], lambda e, i: e.tensor_tensor(
            v196[0:1, :], n0f[0:1, :], lim6[0:1, :], ALU.is_gt))
        once("vector", "v6r", 1, [("v6", None, 1)], lambda e, i: e.tensor_reduce(
            tot[0:1, 4:5], v196[0:1, :], AX.X, ALU.add))

        once("tensor", "pfree", 1, [("keyf", None, 2), ("kvi", None, 2), ("reln", None, 2), ("cmp1", None, 1),
                                    ("wlo", None, 5), ("tot", None, 1)],
             lambda e, i: e.transpose(pp[7][:, 0:128], woS[:, :], ident[:, :]))
        once("vector", "woT", 1, [("pfree", None, 1)], lambda e, i: e.tensor_copy(woT[:, :], pp[7][:, 0:128]))
        for s in range(2):
            once("vector", "stb", 1, [("wlo", None, 5)],
                 lambda e, i, s=s: e.tensor_copy(stq[:, s, :, C:QW], bb[:, :, :]))
        once("tensor", "wgo", 1, [("wl", None, 10), ("woT", None, 1)],
             lambda e, i: e.transpose(pp[7][:, 0:128], ident[:, :], ident[:, :]))

        def lift(e, b, out_, k, r0, r1):
            return e.matmul(out_, xT[:, b * 128:(b + 1) * 128],
                            W[:, k, r0:r1, :].rearrange("p r c -> p (r c)"), start=True, stop=True)

        def parts(ap):
            return ap.rearrange("p (r c) -> p r c", c=C)

        body = [
            ("tensor", "xt", 1, [("xl", None, 2), ("wgo", None, 1), ("xtc", -1)],
             lambda e, b: e.transpose(pp[6][:, 0:128], xs[:, b, :], ident[:, :])),
            ("scalar", "xtc", 1, [("xt", 0)],
             lambda e, b: e.activation(xT[:, b * 128:(b + 1) * 128], pp[6][:, 0:128], ACT.Copy)),
            ("tensor", "pa", 1, [("xtc", 0), ("pk0", -2)], lambda e, b: lift(e, b, pp[b % 2][:, :], 1, 0, 4)),
            ("scalar", "pk0", 1, [("pa", 0), ("tabk", -2)], lambda e, b: e.activation(
                stg[:, b % 2, 0:4, 0:C], parts(pp[b % 2][:, :]), ACT.Copy)),
            ("tensor", "pb", 1, [("pk1", -2)], lambda e, b: lift(e, b, pp[2 + b % 2][:, :], 2, 0, 4)),
            ("vector", "pk1", 1, [("pb", 0), ("tabk", -2)], lambda e, b: e.tensor_copy(
                stg[:, b % 2, 0:4, C:2 * C], parts(pp[2 + b % 2][:, :]))),
            ("tensor", "pc", 1, [("pk2", -2)], lambda e, b: [
                lift(e, b, pp[4 + b % 2][:, 0:C], 1, 4, 5), lift(e, b, pp[4 + b % 2][:, C:2 * C], 2, 4, 5)][1]),
            ("scalar", "pk2", 1, [("pc", 0), ("tabk", -2)], lambda e, b: e.activation(
                stg[:, b % 2, 4, :], pp[4 + b % 2][:, 0:2 * C], ACT.Copy)),
            ("vector", "seek", 1, [("rows", None, NB)], lambda e, b: e.tensor_tensor(
                rowsf[:, b, :], rows[:, b, :], nf[:, b:b + 1].broadcast_to([128, SEEK]), ALU.is_lt)),
            ("vector", "seekr", 1, [("seek", 0)], lambda e, b: e.tensor_reduce(
                cnt2[:, b:b + 1], rowsf[:, b, :], AX.X, ALU.add)),
            ("sync", "tabk", (16, 2), [("pk0", 0), ("pk1", 0), ("pk2", 0)], lambda e, b: e.dma_start(
                KV[b * 640:(b + 1) * 640, :].rearrange("(p r) c -> p (r c)", r=R),
                stg[:, b % 2, :, :].rearrange("p r c -> p (r c)"))),
        ]
        loop(NB, body, False)

        once("vector", "stf", 1, [("seekr", None, NB), ("cnt1", None, 1)], lambda e, i: e.scalar_tensor_tensor(
            stf[:, :], cnt[:, :], float(SEEK), cnt2[:, :], ALU.mult, ALU.add))
        once("vector", "v4", 1, [("stf", None, 1), ("base", None, 1)], lambda e, i: e.tensor_tensor(
            v25[:, 0, :], stf[:, :], base[:, :], ALU.subtract))
        once("vector", "v5", 1, [("v4", None, 1)], lambda e, i: e.tensor_scalar(
            v25[:, 1, :], v25[:, 0, :], 960.0, None, ALU.is_gt))
        once("vector", "v5b", 1, [("v5", None, 1)], lambda e, i: e.tensor_scalar(
            v25[:, 0, :], v25[:, 0, :], -1024.0, None, ALU.is_lt))
        once("vector", "v5r", 1, [("v5b", None, 1)], lambda e, i: e.tensor_reduce(
            tot[0:1, 5:6], v25[0:1, :, :], AX.XY, ALU.add))
        once("vector", "strel0", 1, [("stf", None, 1), ("base", None, 1)], lambda e, i: e.scalar_tensor_tensor(
            strel[:, 1:NB], stf[:, 1:NB], 1024.0, base[:, 1:NB], ALU.add, ALU.subtract))
        once("vector", "strel", 1, [("strel0", None, 1)], lambda e, i: e.tensor_copy(strel[:, 0:1], stf[:, 0:1]))
        once("vector", "totr", 1, [("v5r", None, 1), ("v6r", None, 1), ("tot1", None, 1)], lambda e, i: e.tensor_reduce(
            tot[0:1, 6:7], tot[0:1, 0:6], AX.X, ALU.add))
        once("vector", "flag", 1, [("totr", None, 1)], lambda e, i: e.tensor_scalar(
            flag[:, :], tot[0:1, 6:7], 0.0, None, ALU.is_gt))

        body = [
            ("tensor", "pd", 1, [("wlq", None, 5), ("pk0", None, NB), ("pk1", None, NB), ("pq0", -2)],
             lambda e, b: lift(e, b, pp[b % 2][:, :], 0, 0, 4)),
            (("scalar"), "pq0", 1, [("pd", 0), ("tabq", -2)], lambda e, b: e.activation(
                stq[:, b % 2, 0:4, 0:C], parts(pp[b % 2][:, :]), ACT.Copy, scale=0.25)),
            ("tensor", "pe", 1, [("pq1", -2)], lambda e, b: lift(e, b, pp[2 + b % 2][:, 0:C], 0, 4, 5)),
            ("vector", "pq1", 1, [("pe", 0), ("tabq", -2)], lambda e, b: e.tensor_scalar(
                stq[:, b % 2, 4, 0:C], pp[2 + b % 2][:, 0:C], 0.25, None, ALU.mult)),
            ("sync", "tabq", (16, 2), [("pq0", 0), ("pq1", 0), ("stb", None, 2)], lambda e, b: e.dma_start(
                QT[b * 640:(b + 1) * 640, :].rearrange("(p r) c -> p (r c)", r=R),
                stq[:, b % 2, :, :].rearrange("p r c -> p (r c)"))),
        ]
        loop(NB, body, False)

        slow = Queues(nc, ctx, q)
        general(slow, pp, locals())
        finish(slow, pp, locals())
        quick = Queues(nc, ctx, q)
        fast(quick, pp, locals())

        for one in (q, slow, quick):
            one.number()
        block = ctx.enter_context(nc.Block())

        def run(key, e):
            q.emit(key, e)
            q.steps["flag"].wait(e, 0)
            reg = e.alloc_register("way")
            e.reg_load(reg, flag[0:1, 0:1])
            way = e.snap(reg, min_val=0, max_val=1)
            with e.If(way):
                slow.emit(key, e)
                if key == "sync":
                    for name, n in (("mx0", 1), ("acc0", 1), ("gsm", NT), ("gsa", NT), ("outd", 2)):
                        slow.steps[name].wait_all(e, n)
            with e.Else():
                quick.emit(key, e)
                if key == "sync":
                    for name, n in quick.ends:
                        quick.steps[name].wait_all(e, n)
            if key == "sync":
                q.steps["tabq"].wait_all(e, NB)
                q.steps["tabk"].wait_all(e, NB)

        @block.sync
        def _(e):
            run("sync", e)

        @block.scalar
        def _(e):
            run("scalar", e)

        @block.vector
        def _(e):
            run("vector", e)

        @block.gpsimd
        def _(e):
            run("gpsimd", e)

        @block.tensor
        def _(e):
            run("tensor", e)


def general(q, pp, v):
    once, loop = q.once, q.loop
    KV, QT, MX, ACC = v["KV"], v["QT"], v["MX"], v["ACC"]
    keyf, kvi, ident, pid, aggT = (v[k] for k in ("keyf", "kvi", "ident", "pid", "aggT"))
    room = Region(v["ring"][:, :])

    def sb(name, shape, dt=F32):
        return room.take(shape[1:], dt)

    keyi = sb("g_keyi", [128, NT], U32)
    tri = sb("g_tri", [128, 128])
    once("gpsimd", "tri0", 1, [("flag", None, 1)], lambda e, i: e.memset(tri[:, :], 1.0))
    once("gpsimd", "tri", 1, [("tri0", None, 1)], lambda e, i: e.affine_select(
        out=tri[:, :], in_=tri[:, :], compare_op=ALU.is_gt, fill=0.0, base=0,
        pattern=[[-1, 128]], channel_multiplier=1))
    once("vector", "keyi", 1, [], lambda e, i: e.tensor_copy(keyi[:, :], keyf[:, :]))
    fillm = sb("fillm", [128, H])
    filla = sb("filla", [128, AW])
    kc = sb("g_kc", [128, 1])
    ki = sb("g_ki", [128, 1], U32)
    vi = sb("g_vi", [128, 1], U32)
    gkv = sb("g_kv", [128, 2 * C])
    gq = sb("g_q", [128, QW])
    gm = sb("g_m", [128, H])
    ga = sb("g_a", [128, AW])
    prod = sb("g_prod", [128, C])
    lg = sb("g_lg", [128, H])
    L = sb("g_L", [128, NT * H])
    ne = sb("g_ne", [128, 128])
    eq = sb("g_eq", [128, 128])
    tmp = sb("g_tmp", [128, 128])
    dup = sb("g_dup", [128, 1])
    dfar = sb("g_dfar", [128, 1])
    wf = sb("g_wf", [128, 1])
    wi = sb("g_wi", [128, 1], U32)
    widx = sb("g_widx", [128, NT], U32)
    X = sb("g_X", [128, H, 128])
    mx = sb("g_mx", [128, H])
    ex = sb("g_ex", [128, H])
    EV = sb("g_EV", [128, AW])
    up = sb("g_up", [128, AW])
    KR, LB0, LB1, TT = pp[0][:, 0:128], pp[1], pp[2], pp[3][:, 0:AW]
    at = bass.ds

    def gather(buf, tab, idx):
        return lambda e, i: e.indirect_dma_start(buf[:, :], None, tab, bass.IndirectOffsetOnAxis(idx[:, 0:1], 0))

    def scatter(buf, tab, idx):
        return lambda e, i: e.indirect_dma_start(tab, bass.IndirectOffsetOnAxis(idx[:, 0:1], 0), buf[:, :], None)

    def row_of(col):
        return lambda e, i: e.matmul(KR, col[:, 0:1].broadcast_to([128, 128]), ident[:, :], start=True, stop=True)

    def spread(e, i):
        for h in range(H):
            last = e.matmul((LB0, LB1)[h // 4][:, (h % 4) * 128:(h % 4 + 1) * 128],
                            lg[:, h:h + 1].broadcast_to([128, 128]), ident[:, :], start=True, stop=True)
        return last

    once("vector", "fm", 1, [], lambda e, i: e.memset(fillm[:, :], NEG))
    once("vector", "fa", 1, [], lambda e, i: e.memset(filla[:, :], 0.0))
    once("sync", "mx0", 16, [("fm", None, 1)], lambda e, i: e.dma_start(
        MX.rearrange("(p r) c -> p r c", p=128), fillm[:, None, :].broadcast_to([128, ROWS // 128, H])))
    once("sync", "acc0", 16, [("fa", None, 1)], lambda e, i: e.dma_start(
        ACC.rearrange("(p r) c -> p r c", p=128), filla[:, None, :].broadcast_to([128, ROWS // 128, AW])))
    once("vector", "dfar", 1, [("pid", None, 1)], lambda e, i: e.tensor_scalar(
        dfar[:, :], pid[:, :], float(DUP_ROW), None, ALU.add))

    loop(NT, [
        ("vector", "akc", 1, [("adup", -1), ("awf", -1), ("akr", -1)],
         lambda e, i: e.tensor_copy(kc[:, :], keyf[:, at(i, 1)])),
        ("vector", "aki", 1, [("keyi", None, 1), ("agq", -1), ("agm", -1)],
         lambda e, i: e.tensor_copy(ki[:, :], keyi[:, at(i, 1)])),
        ("vector", "avi", 1, [("agk", -1)],
         lambda e, i: e.tensor_copy(vi[:, :], kvi[:, at(i, 1)])),
        ("gpsimd", "agk", 16, [("avi", 0), ("tabk", None, NB), ("aprod", -1)], gather(gkv, KV, vi)),
        ("gpsimd", "agq", 16, [("aki", 0), ("tabq", None, NB), ("alg", -1)], gather(gq, QT, ki)),
        ("gpsimd", "agm", 16, [("aki", 0), ("mx0", None, 1), ("gsm", -1), ("amx2", -1)], gather(gm, MX, ki)),
        ("tensor", "akr", 1, [("akc", 0), ("id", None, 1), ("aeq", -1), ("pq0", None, NB)], row_of(kc)),
        ("vector", "ane", 1, [("akr", 0), ("akc", 0), ("aX0", -1), ("aX1", -1)], lambda e, i: e.tensor_scalar(
            ne[:, :], KR, kc[:, 0:1], FAR, ALU.not_equal, ALU.mult)),
        ("vector", "aeq", 1, [("akr", 0), ("akc", 0), ("adup", -1)], lambda e, i: e.tensor_scalar(
            eq[:, :], KR, kc[:, 0:1], None, ALU.is_equal)),
        ("vector", "atmp", 1, [("aeq", 0), ("tri", None, 1), ("adup", -1)], lambda e, i: e.tensor_tensor(
            tmp[:, :], eq[:, :], tri[:, :], ALU.mult)),
        ("vector", "adup", 1, [("atmp", 0), ("awf", -1)], lambda e, i: e.tensor_reduce(
            dup[:, :], tmp[:, :], AX.X, ALU.add)),
        ("vector", "adup1", 1, [("adup", 0)], lambda e, i: e.tensor_scalar(
            dup[:, :], dup[:, :], 0.0, None, ALU.is_gt)),
        ("vector", "awf0", 1, [("akc", 0), ("dfar", None, 1), ("awi", -1)], lambda e, i: e.tensor_tensor(
            wf[:, :], dfar[:, :], kc[:, :], ALU.subtract)),
        ("vector", "awf1", 1, [("awf0", 0), ("adup1", 0)], lambda e, i: e.tensor_tensor(
            wf[:, :], wf[:, :], dup[:, :], ALU.mult)),
        ("vector", "awf", 1, [("awf1", 0)], lambda e, i: e.tensor_tensor(
            wf[:, :], wf[:, :], kc[:, :], ALU.add)),
        ("vector", "awi", 1, [("awf", 0), ("gsm", -1)], lambda e, i: e.tensor_copy(wi[:, :], wf[:, :])),
        ("vector", "awx", 1, [("awf", 0)], lambda e, i: e.tensor_copy(widx[:, at(i, 1)], wf[:, :])),
        ("vector", "aprod", 1, [("agk", 0), ("agq", 0), ("alg0", -1)], lambda e, i: e.tensor_tensor(
            prod[:, :], gkv[:, 0:C], gq[:, 0:C], ALU.mult)),
        ("vector", "alg0", 1, [("aprod", 0), ("abc", -1)], lambda e, i: e.tensor_reduce(
            lg[:, :], prod[:, :].rearrange("p (h d) -> p h d", d=D), AX.X, ALU.add)),
        ("vector", "alg", 1, [("alg0", 0), ("agq", 0)], lambda e, i: e.tensor_tensor(
            lg[:, :], lg[:, :], gq[:, C:QW], ALU.add)),
        ("vector", "aL", 1, [("alg", 0)], lambda e, i: e.tensor_copy(L[:, at(i * H, H)], lg[:, :])),
        ("tensor", "abc", 1, [("alg", 0), ("aX0", -1), ("aX1", -1), ("pk1", None, NB)], spread),
        ("vector", "aX0", 1, [("abc", 0), ("ane", 0), ("amx", -1)], lambda e, i: e.tensor_tensor(
            X[:, 0:4, :], LB0[:, :].rearrange("p (h j) -> p h j", h=4),
            ne[:, None, :].broadcast_to([128, 4, 128]), ALU.add)),
        ("vector", "aX1", 1, [("abc", 0), ("ane", 0), ("amx", -1)], lambda e, i: e.tensor_tensor(
            X[:, 4:8, :], LB1[:, :].rearrange("p (h j) -> p h j", h=4),
            ne[:, None, :].broadcast_to([128, 4, 128]), ALU.add)),
        ("vector", "amx", 1, [("aX0", 0), ("aX1", 0), ("gsm", -1)], lambda e, i: e.tensor_reduce(
            mx[:, :], X[:, :, :], AX.X, ALU.max)),
        ("vector", "amx2", 1, [("amx", 0), ("agm", 0)], lambda e, i: e.tensor_tensor(
            mx[:, :], mx[:, :], gm[:, :], ALU.max)),
        ("gpsimd", "gsm", 16, [("amx2", 0), ("awi", 0), ("agm", 0)], scatter(mx, MX, wi)),
    ], True)

    loop(NT, [
        ("vector", "bkc", 1, [("beq", -1), ("bkr", -1), ("gsm", None, NT), ("akr", None, NT), ("abc", None, NT)],
         lambda e, i: e.tensor_copy(kc[:, :], keyf[:, at(i, 1)])),
        ("vector", "bki", 1, [("bgm", -1), ("bga", -1)],
         lambda e, i: e.tensor_copy(ki[:, :], keyi[:, at(i, 1)])),
        ("vector", "bvi", 1, [("bgk", -1)], lambda e, i: e.tensor_copy(vi[:, :], kvi[:, at(i, 1)])),
        ("vector", "bwi", 1, [("gsa", -1), ("awx", None, NT)],
         lambda e, i: e.tensor_copy(wi[:, :], widx[:, at(i, 1)])),
        ("gpsimd", "bgk", 16, [("bvi", 0), ("bev", -1)], gather(gkv, KV, vi)),
        ("gpsimd", "bgm", 16, [("bki", 0), ("bsub", -1)], gather(gm, MX, ki)),
        ("gpsimd", "bga", 16, [("bki", 0), ("acc0", None, 1), ("gsa", -1), ("bup", -1)], gather(ga, ACC, ki)),
        ("tensor", "bkr", 1, [("bkc", 0), ("beq", -1)], row_of(kc)),
        ("vector", "beq", 1, [("bkr", 0), ("bkc", 0), ("btt", -1)], lambda e, i: e.tensor_scalar(
            eq[:, :], KR, kc[:, 0:1], None, ALU.is_equal)),
        ("vector", "bsub", 1, [("bgm", 0), ("bexp", -1), ("aL", None, NT)], lambda e, i: e.tensor_tensor(
            ex[:, :], L[:, at(i * H, H)], gm[:, :], ALU.subtract)),
        ("scalar", "bexp", 1, [("bsub", 0), ("btt", -1)], lambda e, i: e.activation(
            EV[:, C:AW], ex[:, :], ACT.Exp)),
        ("vector", "bev", 1, [("bexp", 0), ("bgk", 0), ("btt", -1)], lambda e, i: e.tensor_tensor(
            EV[:, 0:C].rearrange("p (h d) -> p h d", d=D), gkv[:, C:2 * C].rearrange("p (h d) -> p h d", d=D),
            EV[:, C:AW, None].broadcast_to([128, H, D]), ALU.mult)),
        ("tensor", "btt", 1, [("bev", 0), ("beq", 0), ("bup", -1)], lambda e, i: e.matmul(
            TT, eq[:, :], EV[:, :], start=True, stop=True)),
        ("vector", "bup", 1, [("btt", 0), ("bga", 0), ("gsa", -1)], lambda e, i: e.tensor_tensor(
            up[:, :], ga[:, :], TT, ALU.add)),
        ("gpsimd", "gsa", 16, [("bup", 0), ("bwi", 0), ("bga", 0)], scatter(up, ACC, wi)),
    ], True)

    ca = sb("c_a", [128, R, AW])
    cs = sb("c_s", [128, R, H])
    cg = sb("c_g", [128, C])
    loop(NB, [
        ("sync", "cld", 16, [("gsa", None, NT), ("cmul", -1)], lambda e, b: e.dma_start(
            ca[:, :, :].rearrange("p r c -> p (r c)"),
            ACC[b * 640:(b + 1) * 640, :].rearrange("(p r) c -> p (r c)", r=R))),
        ("vector", "ceps", 1, [("cld", 0), ("cmul", -1)], lambda e, b: e.tensor_scalar(
            cs[:, :, :], ca[:, :, C:AW], 1e-12, None, ALU.add)),
        ("vector", "crec", 1, [("ceps", 0)], lambda e, b: e.reciprocal(cs[:, :, :], cs[:, :, :])),
    ] + [
        ("vector", f"cm{r}", 1, [("crec", 0)], lambda e, b, r=r: e.tensor_tensor(
            ca[:, r, 0:C].rearrange("p (h d) -> p h d", d=D), ca[:, r, 0:C].rearrange("p (h d) -> p h d", d=D),
            cs[:, r, :, None].broadcast_to([128, H, D]), ALU.mult)) for r in range(R)
    ] + [
        ("vector", "cmul", 1, [(f"cm{r}", 0) for r in range(R)] + [("ctr", -1)], lambda e, b: e.tensor_reduce(
            cg[:, :], ca[:, :, 0:C].rearrange("p r c -> p c r"), AX.X, ALU.add)),
        ("tensor", "ctr", 1, [("cmul", 0), ("agg", -1)], lambda e, b: e.transpose(
            pp[4][:, 0:128], cg[:, :], ident[:, :])),
        ("vector", "agg", 1, [("ctr", 0)], lambda e, b: e.tensor_copy(
            aggT[:, b * 128:(b + 1) * 128], pp[4][:, 0:128])),
    ], False)


def finish(q, pp, v):
    loop = q.loop
    xs, aggT, woT, bob, gab, beb, out = (v[k] for k in ("xs", "aggT", "woT", "bob", "gab", "beb", "out"))
    room = Region(v["pool"][:, :])
    res = room.take([NB, C])
    hb = room.take([2, C])
    st = room.take([2, 6])
    mv = room.take([2, 2])
    sd = room.take([2])
    epst = room.take([1])
    q.once("vector", "feps", 1, [], lambda e, i: e.memset(epst[:, :], EPS))

    def stats(p, src, before):
        return [
            ("vector", f"{p}bs", 1, before, lambda e, b: e.bn_stats(st[:, b % 2, :], src(b))),
            ("vector", f"{p}ba", 1, [(f"{p}bs", 0)], lambda e, b: e.bn_aggr(mv[:, b % 2, :], st[:, b % 2, :])),
            ("scalar", f"{p}sq", 1, [(f"{p}ba", 0), ("feps", None, 1)], lambda e, b: e.activation(
                sd[:, b % 2:b % 2 + 1], mv[:, b % 2, 1:2], ACT.Sqrt, bias=epst[:, 0:1])),
            ("vector", f"{p}rc", 1, [(f"{p}sq", 0)], lambda e, b: e.reciprocal(
                sd[:, b % 2:b % 2 + 1], sd[:, b % 2:b % 2 + 1])),
            ("vector", f"{p}nm", 1, [(f"{p}rc", 0)], lambda e, b: e.tensor_scalar(
                src(b), src(b), mv[:, b % 2, 0:1], sd[:, b % 2:b % 2 + 1], ALU.subtract, ALU.mult)),
        ]

    h = lambda b: hb[:, b % 2, :]
    body = [
        ("tensor", "fo", 1, [("agg", None, NB), ("fh0", -1)], lambda e, b: e.matmul(
            pp[6][:, 0:128], aggT[:, b * 128:(b + 1) * 128], woT[:, :], start=True, stop=True)),
        ("vector", "fh0", 1, [("fo", 0), ("fcp", -1)], lambda e, b: e.tensor_tensor(h(b), pp[6][:, 0:128], bob[:, :], ALU.add)),
        ("vector", "fh1", 1, [("fh0", 0)], lambda e, b: e.tensor_tensor(h(b), h(b), xs[:, b, :], ALU.add)),
    ] + stats("f", h, [("fh1", 0)]) + [
        ("vector", "fg", 1, [("fnm", 0)], lambda e, b: e.tensor_tensor(h(b), h(b), gab[:, :], ALU.mult)),
        ("vector", "fb", 1, [("fg", 0)], lambda e, b: e.tensor_tensor(h(b), h(b), beb[:, :], ALU.add)),
        ("vector", "fx", 1, [("fb", 0)], lambda e, b: e.tensor_tensor(h(b), h(b), xs[:, b, :], ALU.add)),
    ] + stats("g", h, [("fx", 0)]) + [
        ("vector", "fcp", 1, [("gnm", 0), ("tabq", None, NB)], lambda e, b: e.tensor_copy(res[:, b, :], h(b))),
    ]
    loop(NB, body, False)
    q.once("sync", "outd", 16, [("fcp", None, NB)], lambda e, i: e.dma_start(
        out[0:3072, :].rearrange("(b p) c -> p b c", p=128), res[:, 0:24, :]))
    q.once("sync", "outd", 16, [("fcp", None, NB)], lambda e, i: e.dma_start(out[3072:N, :], res[0:53, 24, :]))


def fast(q, pp, v):
    q.ends = []
    at = q.at
    ring, xs, aggT, hb, keyf, kvi, relk, reln = (
        v[k] for k in ("ring", "xs", "aggT", "hb", "keyf", "kvi", "relk", "reln"))
    woT, bb, bob, gab, beb, identb, nk, io32, strel, n0i, kbi = (
        v[k] for k in ("woT", "bb", "bob", "gab", "beb", "identb", "nk", "io32", "strel", "n0i", "kbi"))
    pid, KV, QT, CT, LB, out = (v[k] for k in ("pid", "KV", "QT", "CT", "LB", "out"))
    kv = ring[:, :].rearrange("p (s j c) -> p s j c", s=KR, j=4)
    room = Region(v["pool"][:, :])
    ohr = room.take([OR, 4 * C], BF16)
    ohf = room.take([2, 4 * C])
    ab = room.take([2, 4 * C], BF16)
    X = room.take([R, H, SLOTS])
    prod = room.take([4 * C])
    av = room.take([2, 4 * C])
    assert room.off <= 11776
    sb = v["sb"]
    qwin = sb("qwin", [128, 3, C])
    cwin = sb("cwin", [128, 3, 48], BF16)
    ohn = sb("ohn", [128, 2, 4, 32])
    LR = sb("LR", [128, KR, 4, LC])
    lwin = sb("lwin", [128, 2, SLOTS * LC])
    pen = sb("pen", [128, R, SLOTS])
    mxs = sb("mxs", [128, R, H])
    m2 = sb("m2", [128, R, H])
    sm = sb("sm", [128, R, H])
    c16 = sb("c16", [128, R, 16])
    cres = sb("cres", [128, R, 16])
    cst = sb("cst", [128, 2, R, 3, 16], BF16)
    tt = sb("tt", [128, 2, 4, H])
    te = sb("te", [128, 2, 4, H])
    npid = sb("npid", [128, 1])
    one = sb("one", [128, 1])
    epst = sb("epst", [128, 1])
    st = sb("st", [128, 2, 6])
    onesr = sb("onesr", [1, 128])
    mv = sb("mv", [128, 2, 5, 2])
    sd = sb("sd", [128, 2, 5])
    PK = NB * 1

    at("vector", "npid", 1, 0, [("pid", None, 1)], lambda e: e.tensor_scalar(
        npid[:, :], pid[:, :], -1.0, None, ALU.mult))
    at("vector", "one", 1, 0, [], lambda e: e.memset(one[:, :], 1.0))
    at("vector", "onesr", 1, 0, [], lambda e: e.memset(onesr[:, :], 1.0))
    at("vector", "eps", 1, 0, [], lambda e: e.memset(epst[:, :], EPS))
    at("vector", "az", 1, 0, [], lambda e: e.memset(aggT[:, :], 0.0))

    regs = {}

    def values(e, key, table, what, k):
        if k % 8 == 0 or (key, what) not in regs:
            base = k - k % 8
            n = min(8, NQ - base)
            if (key, what) not in regs:
                regs[key, what] = [e.alloc_register(f"{what}{m}") for m in range(8)]
            e.load(regs[key, what][:n], table[0:1, base:base + n])
        top = (N - 1) * (5 if table is kbi else 1)
        return e.snap(regs[key, what][k % 8], min_val=0, max_val=top)

    def gathers(k):
        def emit(e):
            return [e.indirect_dma_start(
                kv[:, k % KR, j, :], None, KV, bass.IndirectOffsetOnAxis(kvi[:, 4 * k + j:4 * k + j + 1], 0))
                for j in range(4)]
        at("gpsimd", "kv", (16, 6, 4), k, [("tabk", None, NB), ("kvi", None, 2), ("av", k - KR), ("prod", k - KR), ("kv", k - 6)]
           + ([("seekr", None, NB)] if k == 0 else []), emit)

    def spread(k):
        def emit(e):
            for j in range(4):
                last = e.matmul(pp[k % 2][:, j * C:(j + 1) * C],
                                relk[:, 4 * k + j:4 * k + j + 1].broadcast_to([128, 128]), identb[:, :],
                                start=True, stop=True)
            return last
        at("tensor", "bc", 1, k, [("relk", None, 1), ("pq0", None, NB), ("abs", k - 2)], emit)
        at("scalar", "abs", 1, k, [("bc", k), ("npid", 0), ("oh2", k - 2), ("tabq", None, NB)],
           lambda e: e.activation(ab[:, k % 2, :], pp[k % 2][:, :], ACT.Abs, bias=npid[:, 0:1]))
        at("scalar", "oh1", 1, k, [("abs", k), ("one", 0), ("qe", k - 2)],
           lambda e: e.activation(ohf[:, k % 2, :], ab[:, k % 2, :], ACT.Relu, bias=one[:, 0:1], scale=-1.0))
        at("scalar", "oh2", 1, k, [("abs", k), ("ce", k - OR)],
           lambda e: e.activation(ohr[:, k % OR, :], ab[:, k % 2, :], ACT.Relu, bias=one[:, 0:1], scale=-1.0))

    def load_q(k):
        at("sync", "qw", (16, 3), k, [("tabq", None, NB), ("kbi", None, 1), ("qe", k - 3)],
           lambda e: e.dma_start(qwin[:, k % 3, :], QT[bass.ds(values(e, "sync", kbi, "kq", k), 128), 0:C]))

    def queries(k):
        def emit(e):
            for j in range(4):
                last = e.matmul(pp[2 + k % 2][:, j * C:(j + 1) * C], ohf[:, k % 2, j * C:(j + 1) * C],
                                qwin[:, k % 3, :], start=True, stop=True)
            return last
        at("tensor", "qe", 1, k, [("oh1", k), ("qw", k), ("prod", k - 2)], emit)

    def holders(k):
        return [b for b in range(NB) if first_quad(b) <= k <= last_quad(b)]

    written = {}

    def logits(k, part):
        used = [(f"lb{b}", None, last_quad(b) - first_quad(b) + 1) for b in holders(k - KR)] if k >= KR else []
        if part == 0:
            at("vector", "prod", 1, k, [("qe", k), ("kv", k), ("red", k - 1)], lambda e: e.tensor_tensor(
                prod[:, :].rearrange("p (j c) -> p j c", j=4), pp[2 + k % 2][:, :].rearrange("p (j c) -> p j c", j=4),
                kv[:, k % KR, :, 0:C], ALU.mult))
        elif part == 1:
            at("vector", "red", 1, k, [("prod", k), ("ta", k - KR)] + used, lambda e: e.tensor_reduce(
                LR[:, k % KR, :, 0:H], prod[:, :].rearrange("p (j h d) -> p j h d", j=4, d=D), AX.X, ALU.add))
        elif part == 2:
            at("vector", "kc", 1, k, [("keyf", None, 2)] + used, lambda e: e.tensor_copy(
                LR[:, k % KR, :, H], keyf[:, 4 * k:4 * k + 4]))
        else:
            for b in holders(k):
                t = written.get(b, 0)
                written[b] = t + 1
                f = (k - first_quad(b)) * 512
                at("sync", f"lb{b}", 16, t, [("red", k), ("kc", k)], lambda e, b=b, f=f: e.dma_start(
                    LB[b][f:f + 512, :].rearrange("(p j) c -> p (j c)", j=4),
                    LR[:, k % KR, :, :].rearrange("p j c -> p (j c)")))

    def fetch(b):
        n = last_quad(b) - first_quad(b) + 1
        at("gpsimd", "sg", (16, 2), b, [(f"lb{b}", None, n), ("xa4", b - 2), ("strel", None, 1)],
           lambda e: e.indirect_dma_start(lwin[:, b % 2, :], None, LB[b], bass.IndirectOffsetOnAxis(strel[:, b:b + 1], 0)))

    def maxima(b, r, part):
        win = lwin[:, b % 2, :].rearrange("p (j c) -> p c j", c=LC)
        if part == 0:
            at("vector", f"pen{r}", 1, b, [("sg", b), (f"xa{r}", b - 1), ("nk", None, 1)], lambda e: e.tensor_scalar(
                pen[:, r, :], win[:, H, :], nk[:, r, b:b + 1], FAR, ALU.not_equal, ALU.mult))
        elif part == 1:
            at("vector", f"xa{r}", 1, b, [(f"pen{r}", b), (f"ex{r}", b - 1)], lambda e: e.tensor_tensor(
                X[:, r, :, :], win[:, 0:H, :], pen[:, r, None, :].broadcast_to([128, H, SLOTS]), ALU.add))
        elif part == 2:
            at("vector", f"xm{r}", 1, b, [(f"xa{r}", b), (f"ms{r}", b - 1)], lambda e: e.tensor_reduce(
                mxs[:, r, :], X[:, r, :, :], AX.X, ALU.max))
        elif part == 3:
            at("vector", f"ms{r}", 1, b, [(f"xm{r}", b), (f"mt{r}", b - 1)], lambda e: e.tensor_tensor(
                m2[:, r, :], mxs[:, r, :], bb[:, r, :], ALU.add))
        elif part == 4:
            at("vector", f"mt{r}", 1, b, [(f"ms{r}", b), (f"ex{r}", b - 1), ("cl1", b - 1)],
               lambda e: e.scalar_tensor_tensor(
                   c16[:, r, 0:H], m2[:, r, :], NEG, bb[:, r, :], ALU.max, ALU.subtract))
        else:
            at("vector", f"mu{r}", 1, b, [(f"mt{r}", b)], lambda e: e.tensor_scalar(
                c16[:, r, 0:H], c16[:, r, 0:H], -1.0, None, ALU.mult))

    def exps(b, r):
        def emit(e):
            return [e.activation(X[:, r, h, :], X[:, r, h, :], ACT.Exp, bias=c16[:, r, h:h + 1],
                                 accum_out=sm[:, r, h:h + 1]) for h in range(H)]
        at("scalar", f"ex{r}", (1, 1, H), b, [(f"mu{r}", b), (f"xm{r}", b), ("ra", b - 1)], emit)

    def constants(b):
        at("vector", "ra", 1, b, [(f"ex{r}", b) for r in range(R)], lambda e: e.tensor_scalar(
            c16[:, :, H:16], sm[:, :, :], 1e-12, None, ALU.add))
        at("vector", "rb", 1, b, [("ra", b)], lambda e: e.reciprocal(c16[:, :, H:16], c16[:, :, H:16]))
        cs = cst[:, b % 2, :, :, :]
        at("vector", "ch", 1, b, [("rb", b), ("cw", b - 2)], lambda e: e.tensor_copy(cs[:, :, 0, :], c16[:, :, :]))
        at("vector", "cl0", 1, b, [("ch", b)], lambda e: e.tensor_tensor(
            cres[:, :, :], c16[:, :, :], cs[:, :, 0, :], ALU.subtract))
        at("vector", "cm", 1, b, [("cl0", b)], lambda e: e.tensor_copy(cs[:, :, 1, :], cres[:, :, :]))
        at("vector", "cl1", 1, b, [("cm", b)], lambda e: e.tensor_tensor(
            cs[:, :, 2, :], cres[:, :, :], cs[:, :, 1, :], ALU.subtract))
        at("sync", "cw", (16, 2), b, [("cl1", b)], lambda e: e.dma_start(
            CT[b * 640:(b + 1) * 640, :].rearrange("(p r) c -> p (r c)", r=R),
            cs.rearrange("p r m c -> p (r m c)")))

    def load_c(k):
        n = last_block(k) + 1
        at("sync", "cl", (16, 3), k, [("cw", None, n), ("kbi", None, 1), ("ce", k - 3)],
           lambda e: e.dma_start(cwin[:, k % 3, :], CT[bass.ds(values(e, "sync", kbi, "kc", k), 128), :]))

    def bring(k):
        def emit(e):
            for j in range(4):
                for m in range(3):
                    last = e.matmul(pp[4 + k % 2][:, j * 16:(j + 1) * 16], ohr[:, k % OR, j * C:(j + 1) * C],
                                    cwin[:, k % 3, m * 16:(m + 1) * 16], start=(m == 0), stop=(m == 2))
            return last
        at("tensor", "ce", 1, k, [("oh2", k), ("cl", k), ("atn", k - 2)], emit)

    def consts_of(k, lo):
        return pp[4 + k % 2][:, 0:64].rearrange("p (j c) -> p j c", j=4)[:, :, lo:lo + H]

    def shift(k):
        at("vector", "ta", 1, k, [("ce", k), ("te", k - 2), ("red", k)], lambda e: e.tensor_tensor(
            tt[:, k % 2, :, :], LR[:, k % KR, :, 0:H], consts_of(k, 0), ALU.add))
        at("scalar", "te", 1, k, [("ta", k), ("atn", k - 2)], lambda e: e.activation(
            te[:, k % 2, :, :], tt[:, k % 2, :, :], ACT.Exp))

    def weigh(k, part):
        if part == 0:
            at("vector", "on", 1, k, [("reln", None, 2), ("io32", None, 1), ("ag", k - 2)], lambda e: e.tensor_tensor(
                ohn[:, k % 2, :, :], reln[:, 4 * k:4 * k + 4, None].broadcast_to([128, 4, 32]),
                io32[:, None, :].broadcast_to([128, 4, 32]), ALU.is_equal))
        elif part == 1:
            at("vector", "atn", 1, k, [("te", k), ("av", k - 2)], lambda e: e.tensor_tensor(
                te[:, k % 2, :, :], te[:, k % 2, :, :], consts_of(k, H), ALU.mult))
        else:
            at("vector", "av", 1, k, [("atn", k), ("ag", k - 2)], lambda e: e.tensor_tensor(
                av[:, k % 2, :].rearrange("p (j h d) -> p j h d", j=4, d=D),
                kv[:, k % KR, :, C:2 * C].rearrange("p j (h d) -> p j h d", d=D),
                te[:, k % 2, :, :, None].broadcast_to([128, 4, H, D]), ALU.mult))

    def collect(k):
        def emit(e):
            for j in range(4):
                last = e.matmul(pp[6 + k % 2][:, 0:32], av[:, k % 2, j * C:(j + 1) * C], ohn[:, k % 2, j, :],
                                start=(j == 0), stop=(j == 3))
            return last
        at("tensor", "ag", 1, k, [("av", k), ("on", k), ("aa", k - 2)]
           + [("h0", b) for b in range(NB) if last_quad(b) + 1 == k - 2], emit)

    def gather_in(k):
        def emit(e):
            to = aggT[:, bass.ds(values(e, "vector", n0i, "na", k), 32)]
            return e.tensor_tensor(to, to, pp[6 + k % 2][:, 0:32], ALU.add)
        at("vector", "aa", 1, k, [("ag", k), ("az", 0), ("aa", k - 1), ("n0i", None, 1)], emit)

    def project(b):
        P = pp[6 + (last_quad(b) + 1) % 2][:, 128:256]
        m = b % 5

        def emit(e):
            e.matmul(P, aggT[:, b * 128:(b + 1) * 128], woT[:, :], start=True, stop=False)
            return e.matmul(P, onesr[0:1, :], bob[0:1, :], start=False, stop=True)
        at("tensor", "fo", 1, b, [("aa", min(last_quad(b) + 1, NQ - 1)), ("woT", None, 1), ("h0", b - 1),
                                  ("onesr", 0)], emit)
        at("vector", "h0", 1, b, [("fo", b)] + ([("n2", b - 5), ("od", b // 5 - 1)] if b >= 5 else []),
           lambda e: e.tensor_tensor(hb[:, m, :], P, xs[:, b, :], ALU.add))

    def project_stats(b):
        m = b % 5
        at("vector", "b1", 1, b, [("h0", b)], lambda e: e.bn_stats(st[:, 0, :], hb[:, m, :]))
        at("vector", "b2", 1, b, [("b1", b)], lambda e: e.bn_aggr(mv[:, 0, m, :], st[:, 0, :]))

    def root(g, n):
        at("scalar", f"q{n}", 1, g, [(f"b{2 * n}", 5 * g + 4), ("eps", 0)], lambda e: e.activation(
            sd[:, n - 1, :], mv[:, n - 1, :, 1], ACT.Sqrt, bias=epst[:, 0:1]))
        at("vector", f"r{n}", 1, g, [(f"q{n}", g)], lambda e: e.reciprocal(sd[:, n - 1, :], sd[:, n - 1, :]))

    def norm1(b, part):
        g, m = b // 5, b % 5
        y = hb[:, m, :]
        if part == 0:
            at("vector", "n1", 1, b, [("r1", g)], lambda e: e.scalar_tensor_tensor(
                y, y, mv[:, 0, m, 0:1], gab[:, :], ALU.subtract, ALU.mult))
        elif part == 1:
            at("vector", "g1", 1, b, [("n1", b)], lambda e: e.scalar_tensor_tensor(
                y, y, sd[:, 0, m:m + 1], xs[:, b, :], ALU.mult, ALU.add))
        elif part == 2:
            at("vector", "g2", 1, b, [("g1", b)], lambda e: e.tensor_tensor(y, y, beb[:, :], ALU.add))
        elif part == 3:
            at("vector", "b3", 1, b, [("g2", b)], lambda e: e.bn_stats(st[:, 1, :], y))
        else:
            at("vector", "b4", 1, b, [("b3", b)], lambda e: e.bn_aggr(mv[:, 1, m, :], st[:, 1, :]))

    def norm2(g):
        for m in range(5):
            at("vector", "n2", 1, 5 * g + m, [("r2", g)], lambda e, m=m: e.tensor_scalar(
                hb[:, m, :], hb[:, m, :], mv[:, 1, m, 0:1], sd[:, 1, m:m + 1], ALU.subtract, ALU.mult))
        if g < 4:
            at("sync", "od", 16, g, [("n2", 5 * g + 4)], lambda e: e.dma_start(
                out[640 * g:640 * (g + 1), :].rearrange("(b p) c -> p b c", p=128), hb[:, :, :]))
        else:
            at("sync", "od", 16, 4, [("n2", 24)], lambda e: e.dma_start(
                out[2560:3072, :].rearrange("(b p) c -> p b c", p=128), hb[:, 0:4, :]))
            at("sync", "od", 16, 5, [("n2", 24)], lambda e: e.dma_start(out[3072:N, :], hb[0:53, 4, :]))

    for k in range(PF):
        gathers(k)
        load_q(k)
    spread(0)
    spread(1)
    queries(0)
    S = NQ + LAG + 16
    ready = {8 * b + 9: b for b in range(NB)}
    done = {max(last_quad(b) + LAG + 3, 8 * b + LAG + 12): b for b in range(NB)}
    last = {s: b // 5 for s, b in done.items() if b % 5 == 4}
    for s in range(S):
        c = s - LAG
        if s + PF < NQ:
            gathers(s + PF)
        if s - 1 in ready:
            fetch(ready[s - 1])
        stats = [(ready[s - 2 - r], r) for r in range(R) if s - 2 - r in ready]
        norms = [(5 * last[s - 2 - m] + m) for m in range(5) if s - 2 - m in last]

        def share(part):
            for b, r in stats:
                maxima(b, r, part)
            for b in norms:
                if part < 5:
                    norm1(b, part)

        if s + PF < NQ:
            load_q(s + PF)
        if 0 <= c + 1 < NQ:
            load_c(c + 1)
        if 0 <= c < NQ:
            bring(c)
            shift(c)
        if s + 2 < NQ:
            spread(s + 2)
        if s + 1 < NQ:
            queries(s + 1)
        if 0 <= c - 1 < NQ:
            collect(c - 1)
        if s - 8 in ready:
            constants(ready[s - 8])
        if s - 2 in last:
            root(last[s - 2], 1)
        if s < NQ:
            logits(s, 0)
        share(0)
        if 0 <= c < NQ:
            weigh(c, 0)
        if s < NQ:
            logits(s, 1)
        share(1)
        if 0 <= c < NQ:
            weigh(c, 1)
        if s < NQ:
            logits(s, 2)
            logits(s, 3)
        share(2)
        if 0 <= c < NQ:
            weigh(c, 2)
        share(3)
        if 0 <= c - 1 < NQ:
            gather_in(c - 1)
        share(4)
        if s in done:
            project(done[s])
        share(5)
        if s - 1 in done:
            project_stats(done[s - 1])
        for b, r in [(ready[s - 3 - r], r) for r in range(R) if s - 3 - r in ready]:
            exps(b, r)
        if s - 7 in last:
            root(last[s - 7], 2)
            norm2(last[s - 7])
    q.ends = [(f"lb{b}", last_quad(b) - first_quad(b) + 1) for b in range(NB)] + [("cw", NB), ("od", 6)]




_INS = ["x", "src", "dst", "edge_type_5", "L0_gnn_W_Q", "L0_gnn_W_K", "L0_gnn_W_V", "L0_gnn_attn_bias",
        "L0_gnn_out_proj_w", "L0_gnn_out_proj_b", "L0_gnn_ln_gamma", "L0_gnn_ln_beta"]


def kernel(**inputs):
    import numpy as np
    import concourse.bacc as bacc
    from concourse.bass_utils import run_bass_kernel_spmd

    nc = bacc.Bacc("TRN2", target_bir_lowering=False, num_devices=1)
    arrays, args = {}, []
    for name in _INS:
        a = np.ascontiguousarray(inputs[name])
        arrays["in_" + name] = a
        args.append(nc.dram_tensor("in_" + name, a.shape, mybir.dt.from_np(a.dtype), kind="ExternalInput").ap())
    args.append(nc.dram_tensor("out_0", (N, C), F32, kind="ExternalOutput").ap())
    build(nc, *args)
    r = run_bass_kernel_spmd(nc, [arrays], core_ids=[0])
    return r.results[0]["out_0"]
```

```python
import concourse.bass as bass
from concourse import mybir
from contextlib import ExitStack

N = 3125
E = 100000
R = 5
H = 8
D = 16
C = 128
NB = 25
NQ = 196
HQ = 98
NT = 4 * NQ
KEYS = N * R
DUP_ROW = KEYS + 128
ROWS = 16128
QW = C + H
AW = C + H
NEG = -1.0e9
FAR = -1.0e30
EPS = 1e-5
SPAN = 24
SLOTS = 64
LC = H + 1
LAG = 23
KR = 27
OR = 25
PF = 3
SEEK = 250
POOL = 10304
TURNS = (3, 6, 9, 13, 16)
EARLY = (17, 18, 19, 20)
NORMS = (3, 4, 5, 11, 12)
FETCH = 2
CATCH = 999
DOUBLE = (2,)

F32 = mybir.dt.float32
BF16 = mybir.dt.bfloat16
I32 = mybir.dt.int32
U32 = mybir.dt.uint32
ALU = mybir.AluOpType
ACT = mybir.ActivationFunctionType
AX = mybir.AxisListType


def first_quad(b):
    return max(8 * b - 2, 0)


def last_quad(b):
    return min(8 * b + 9, NQ - 1)


def last_block(q):
    return min((16 * q + 58) // 128, NB - 1)


class Own:

    def __init__(self, sems, inc, per):
        self.sems = sems
        self.inc = inc
        self.per = per

    def wait(self, eng, turn):
        n = len(self.sems)
        if n == 1:
            eng.wait_ge(self.sems[0], (turn + 1) * (self.inc * self.per))
        else:
            eng.wait_ge(self.sems[turn % n], (turn // n + 1) * self.inc * self.per)

    def wait_all(self, eng, times):
        for t in range(max(times - len(self.sems), 0), times):
            self.wait(eng, t)

    def end(self, ins, i):
        sem = self.sems[0] if len(self.sems) == 1 else self.sems[i % len(self.sems)]
        for one in ins if isinstance(ins, list) else [ins]:
            one.then_inc(sem, self.inc)


class Counted:

    def __init__(self, sem, per):
        self.sem = sem
        self.per = per
        self.values = []

    def wait(self, eng, turn):
        eng.wait_ge(self.sem, self.values[turn])

    def wait_all(self, eng, times):
        self.wait(eng, times - 1)

    def end(self, ins, i):
        for one in ins if isinstance(ins, list) else [ins]:
            one.then_inc(self.sem, 1)


class Queues:

    def __init__(self, nc, ctx, parent=None):
        self.nc = nc
        self.ctx = ctx
        self.parent = parent
        self.steps = dict(parent.steps) if parent else {}
        names = ("scalar", "vector", "gpsimd", "tensor")
        self.tick = parent.tick if parent else ctx.enter_context(nc.semaphore("tick"))
        self.counts = parent.counts if parent else {k: ctx.enter_context(nc.semaphore("n_" + k)) for k in names}
        self.count = {}
        self.lists = {"sync": [], "scalar": [], "vector": [], "gpsimd": [], "tensor": []}

    def step(self, eng, name, inc, rolled):
        if name in self.steps:
            return
        inc, n, per = (*inc, 1)[:3] if isinstance(inc, tuple) else (inc, 1, 1)
        if inc == 1 and not rolled:
            self.steps[name] = Counted(self.counts[eng], per)
        else:
            self.steps[name] = Own([self.ctx.enter_context(self.nc.semaphore(f"s_{name}_{k}")) for k in range(n)],
                                   inc, per)

    def loop(self, count, body, rolled):
        for eng, name, inc, _, _ in body:
            self.step(eng, name, inc, rolled)
        for key in self.lists:
            mine = [b for b in body if b[0] == key]
            if not mine:
                continue
            if rolled:
                self.lists[key].append((None, mine, count))
            else:
                for i in range(count):
                    for _, name, inc, after, emit in mine:
                        fixed = [a if len(a) == 3 else (a[0], i + a[1]) for a in after]
                        self.lists[key].append((i, name, fixed, lambda e, i=i, emit=emit: emit(e, i)))

    def once(self, eng, name, inc, after, emit):
        self.step(eng, name, inc, False)
        self.lists[eng].append((-1, name, after, lambda e: emit(e, 0)))

    def at(self, eng, name, inc, turn, after, emit):
        self.step(eng, name, inc, False)
        self.lists[eng].append((turn, name, after, emit))

    def number(self):
        self.count = dict(self.parent.count) if self.parent else dict.fromkeys(self.lists, 0)
        for key, entries in self.lists.items():
            for turn, name, *_ in entries:
                if turn is not None and isinstance(self.steps[name], Counted):
                    one = self.steps[name]
                    self.count[key] += one.per
                    assert turn in (-1, len(one.values)), (name, turn, len(one.values))
                    one.values.append(self.count[key])

    def turn(self, eng, mine, i, key):
        for _, name, _, after, emit in mine:
            for a in after:
                if len(a) == 3:
                    self.steps[a[0]].wait_all(eng, a[2])
                elif a[1] == 0 or not isinstance(i, int) or i + a[1] >= 0:
                    self.steps[a[0]].wait(eng, i + a[1])
            if key == "gpsimd":
                eng.sem_inc(self.tick, 1)
            self.steps[name].end(emit(eng, i), i)

    def emit(self, key, eng):
        for entry in self.lists[key]:
            if entry[0] is None:
                _, mine, count = entry
                self.turn(eng, mine, 0, key)
                with eng.Fori(1, count) as i:
                    self.turn(eng, mine, i, key)
                continue
            turn, name, after, emit = entry
            for a in after:
                if len(a) == 3:
                    self.steps[a[0]].wait_all(eng, a[2])
                elif a[1] >= 0:
                    self.steps[a[0]].wait(eng, a[1])
            self.steps[name].end(emit(eng), max(turn, 0))


class Region:

    def __init__(self, ap):
        self.ap = ap
        self.off = 0

    def take(self, shape, dt=F32, parts=128):
        n = 1
        for k in shape:
            n *= k
        words = n if dt not in (BF16,) else (n + 1) // 2
        a = self.ap[0:parts, self.off:self.off + words]
        self.off += words
        if dt != F32:
            a = a.bitcast(dt)
        names = "abcde"[:len(shape)]
        if len(shape) > 1:
            a = a.rearrange(f"p ({' '.join(names)}) -> p {' '.join(names)}",
                            **{m: k for m, k in zip(names, shape)})
        return a


def build(nc, x, src, dst, typ, wqs, wk, wv, bias, wo, bo, gamma, beta, out):
    ctx = ExitStack()
    with ctx:
        def sb(name, shape, dt=F32):
            return ctx.enter_context(nc.sbuf_tensor(name, shape, dt))

        def ps(name, shape, dt=F32):
            return ctx.enter_context(nc.psum_tensor(name, shape, dt))

        KV = nc.dram_tensor("KVtab", [NB * 640, 2 * C], F32).ap()
        QT = nc.dram_tensor("Qtab", [NB * 640, QW], F32).ap()
        QF = nc.dram_tensor("Qfast", [NB * 640, 3 * C], BF16).ap()
        MX = nc.dram_tensor("MXtab", [ROWS, H], F32).ap()
        ACC = nc.dram_tensor("ACCtab", [ROWS, AW], F32).ap()
        CT = nc.dram_tensor("Ctab", [NB * 640, 48], BF16).ap()
        LB = [nc.dram_tensor(f"Ltab{b}", [(last_quad(b) - first_quad(b) + 1) * 512, LC], F32).ap() for b in range(NB)]

        ring = sb("ring", [128, KR * 4 * 2 * C])
        pool = sb("pool", [128, POOL])
        wq = sb("wq", [128, R, C])
        xs = sb("xs", [128, NB, C])
        aggT = sb("aggT", [128, NB * 128 + 32])
        hb = sb("hb", [128, 10, C])
        keyf = sb("keyf", [128, NT])
        kvi = sb("kvi", [128, NT], U32)
        relk = sb("relk", [128, NT], BF16)
        reln = sb("reln", [128, NT], BF16)
        woT = sb("woT", [128, C])
        bb = sb("bb", [128, R, H])
        bob = sb("bob", [128, C])
        gab = sb("gab", [128, C])
        beb = sb("beb", [128, C])
        ident = sb("ident", [128, 128])
        identb = sb("identb", [128, 128], BF16)
        negb = sb("negb", [128, 128], BF16)
        pid = sb("pid", [128, 1])
        nk = sb("nk", [128, R, NB])
        io32 = sb("io32", [128, 32], BF16)
        strel = sb("strel", [128, NB], U32)
        n0i = sb("n0i", [1, NQ], I32)
        kbi = sb("kbi", [1, NQ], I32)
        flag = sb("flag", [1, 1], I32)
        pp = [ps(f"pp{i}", [128, 512]) for i in range(8)]

        early = Region(pool[:, :])
        xT = early.take([NB * 128])
        W = early.take([2, R, C])
        stg = early.take([2, R, 2 * C])
        stq = early.take([2, R, QW])
        eqb = early.take([R, 3, C], BF16)
        assert early.off <= POOL
        temp = Region(ring[:, :])
        natd = temp.take([2, 577], I32, HQ)
        nats = temp.take([2, 512], I32, HQ)
        natt = temp.take([2, 512], I32, HQ)
        fd = temp.take([2, 577], F32, HQ)
        fs = temp.take([2, 512], F32, HQ)
        ft = temp.take([2, 512], F32, HQ)
        junk = natd.bitcast(F32)[:, :, 0:576]
        far5 = temp.take([4, 2], I32, 100)
        far5f = temp.take([4, 2], F32, 100)
        cmp1 = temp.take([NB + 1, 400])
        woS = temp.take([C])
        rows = temp.take([NB, SEEK], I32)
        rowsf = rows.bitcast(F32)
        nf = temp.take([NB])
        cnt = temp.take([NB])
        qi = temp.take([NB], U32)
        cnt2 = temp.take([NB])
        stf = temp.take([NB])
        n0f = temp.take([NQ])
        t4 = temp.take([NQ, 4])
        viol = temp.take([4], F32, HQ)
        v196 = temp.take([NQ])
        lim6 = temp.take([NQ])
        v25 = temp.take([2, NB])
        tot = temp.take([8])
        ones = temp.take([1])
        base = temp.take([NB])
        eqs = temp.take([R, C])
        eqr = temp.take([R, C])

        q = Queues(nc, ctx)
        once, loop = q.once, q.loop

        once("gpsimd", "id0", 1, [], lambda e, i: e.memset(ident[:, :], 0.0))
        once("gpsimd", "id", 1, [("id0", None, 1)], lambda e, i: e.affine_select(
            out=ident[:, :], in_=ident[:, :], compare_op=ALU.not_equal, fill=1.0, base=0,
            pattern=[[-1, 128]], channel_multiplier=1))
        once("gpsimd", "pid", 1, [], lambda e, i: e.iota(
            pid[:, :], [[0, 1]], base=0, channel_multiplier=1, allow_small_or_imprecise_dtypes=True))
        once("gpsimd", "nf", 1, [], lambda e, i: e.iota(
            nf[:, :], [[128, NB]], base=0, channel_multiplier=1, allow_small_or_imprecise_dtypes=True))
        once("gpsimd", "nk", 1, [], lambda e, i: e.iota(
            nk[:, :, :], [[1, R], [640, NB]], base=0, channel_multiplier=5, allow_small_or_imprecise_dtypes=True))
        once("gpsimd", "io32", 1, [], lambda e, i: e.iota(
            io32[:, :], [[1, 32]], base=0, channel_multiplier=0, allow_small_or_imprecise_dtypes=True))
        once("gpsimd", "base", 1, [], lambda e, i: e.iota(
            base[:, :], [[4096, NB]], base=0, channel_multiplier=0, allow_small_or_imprecise_dtypes=True))
        once("gpsimd", "ones", 1, [], lambda e, i: e.memset(ones[:, :], 1.0))
        edge = 0
        for b in range(NB):
            end = edge
            while end < NQ and last_block(end) == b:
                end += 1
            if end > edge:
                once("gpsimd", "lim6", 1, [], lambda e, i, a=edge, z=end, b=b: e.memset(
                    lim6[:, a:z], float(128 * (b + 1) - 26)))
            edge = end
        once("vector", "nz", 1, [], lambda e, i: e.memset(natd[:, :, :], N))
        once("vector", "nz", 1, [], lambda e, i: e.memset(nats[:, 1, :], 0))
        once("vector", "nz", 1, [], lambda e, i: e.memset(natt[:, 1, :], 0))
        once("vector", "xz", 1, [], lambda e, i: e.memset(xs[:, 24, :], 0.0))

        once("sync", "far", 16, [], lambda e, i: e.dma_start(
            far5[:, :, :], dst.rearrange("(c r s) -> r c s", c=4, s=SEEK)[:, :, 0:2]))
        once("sync", "nat", 16, [("nz", None, 3)], lambda e, i: e.dma_start(
            natd[0:98, 0, 0:512], dst[0:HQ * 512].rearrange("(r c) -> r c", c=512)))
        once("sync", "nat", 16, [("nz", None, 3)], lambda e, i: e.dma_start(
            natd[0:98, 0, 512:577], dst[512:512 + HQ * 512].rearrange("(r c) -> r c", c=512)[:, 0:65]))
        once("sync", "nat", 16, [("nz", None, 3)], lambda e, i: e.dma_start(
            natd[0:97, 1, 0:512], dst[HQ * 512:195 * 512].rearrange("(r c) -> r c", c=512)))
        once("sync", "nat", 16, [("nz", None, 3)], lambda e, i: e.dma_start(
            natd[0:96, 1, 512:577], dst[99 * 512:195 * 512].rearrange("(r c) -> r c", c=512)[:, 0:65]))
        once("sync", "nat", 16, [("nz", None, 3)], lambda e, i: e.dma_start(
            natd[96:97, 1, 512:577], dst[195 * 512:195 * 512 + 65].rearrange("(r c) -> r c", r=1)))
        once("sync", "nat", 16, [("nz", None, 3)], lambda e, i: e.dma_start(
            natd[97:98, 1, 0:160], dst[195 * 512:E].rearrange("(r c) -> r c", r=1)))
        for t, a in ((nats, src), (natt, typ)):
            once("sync", "nst", 16, [], lambda e, i, t=t, a=a: e.dma_start(
                t[0:98, 0, :], a[0:HQ * 512].rearrange("(r c) -> r c", c=512)))
            once("sync", "nst", 16, [("nz", None, 3)], lambda e, i, t=t, a=a: e.dma_start(
                t[0:97, 1, :], a[HQ * 512:195 * 512].rearrange("(r c) -> r c", c=512)))
            once("sync", "nst", 16, [("nz", None, 3)], lambda e, i, t=t, a=a: e.dma_start(
                t[97:98, 1, 0:160], a[195 * 512:E].rearrange("(r c) -> r c", r=1)))
        once("scalar", "xl", 16, [], lambda e, i: e.dma_start(
            xs[:, 0:24, :], x[0:3072, :].rearrange("(b p) c -> p b c", p=128)))
        once("scalar", "xl", 16, [("xz", None, 1)], lambda e, i: e.dma_start(xs[0:53, 24, :], x[3072:N, :]))
        for k, a in ((0, wk), (1, wv), (2, wqs)):
            once("scalar", "wl" if k < 2 else "wlq", 16, [], lambda e, i, k=k, a=a: e.dma_start(
                (wq if k == 2 else W[:, k, :, :]).rearrange("p r (k d) -> p (r k) d", d=D),
                a.rearrange("r k h d -> h (r k) d")))
        once("scalar", "wlo", 16, [], lambda e, i: e.dma_start(woS[:, :], wo))
        once("scalar", "wlo", 16, [], lambda e, i: e.dma_start(
            bb[:, :, :].rearrange("p r h -> p (r h)"),
            bias.rearrange("r h -> (r h)").partition_broadcast(128)))
        for dst_, a in ((bob, bo), (gab, gamma), (beb, beta)):
            once("scalar", "wlo", 16, [], lambda e, i, d=dst_, a=a: e.dma_start(d[:, :], a.partition_broadcast(128)))

        once("vector", "f5", 1, [("far", None, 1)], lambda e, i: e.tensor_copy(far5f[:, :, :], far5[:, :, :]))
        once("vector", "idb", 1, [("id", None, 1)], lambda e, i: e.tensor_copy(identb[:, :], ident[:, :]))
        once("vector", "idn", 1, [("id", None, 1)], lambda e, i: e.tensor_scalar(
            negb[:, :], ident[:, :], -1.0, None, ALU.mult))
        for c in range(4):
            once("tensor", "f5b", 1, [("f5", None, 1), ("id", None, 1)], lambda e, i, c=c: e.matmul(
                pp[6][:, c * 100:(c + 1) * 100], far5f[:, c, 0:1].broadcast_to([100, 128]), ident[0:100, 0:100],
                start=True, stop=True))
        once("vector", "cmp", 1, [("f5b", None, 4)], lambda e, i: e.tensor_copy(cmp1[:, 0, :], pp[6][:, 0:400]))
        for b in range(NB):
            once("vector", "cnt", 1, [("cmp", None, 1), ("nf", None, 1)], lambda e, i, b=b: e.tensor_scalar(
                cmp1[:, 1 + b, :], cmp1[:, 0, :], nf[:, b:b + 1], None, ALU.is_lt, op1=ALU.add,
                accum_out=cnt[:, b:b + 1]))
        once("vector", "cnt1", 1, [("cnt", None, NB)], lambda e, i: e.tensor_scalar(
            cnt[:, :], cnt[:, :], -1.0, 0.0, ALU.add, ALU.max))
        once("vector", "qi", 1, [("cnt1", None, 1)], lambda e, i: e.tensor_copy(qi[:, :], cnt[:, :]))
        for b in range(NB):
            once("gpsimd", "rows", (16, 1), [("qi", None, 1)], lambda e, i, b=b: e.indirect_dma_start(
                rows[:, b, :], None, dst.rearrange("(r c) -> r c", c=SEEK),
                bass.IndirectOffsetOnAxis(qi[:, b:b + 1], 0)))
        once("vector", "fd", 1, [("nat", None, 6)], lambda e, i: e.tensor_copy(fd[:, :, :], natd[:, :, :]))
        once("vector", "fs", 1, [("nst", None, 6)], lambda e, i: e.tensor_copy(fs[:, :, :], nats[:, :, :]))
        once("vector", "ft", 1, [("nst", None, 6)], lambda e, i: e.tensor_copy(ft[:, :, :], natt[:, :, :]))
        once("vector", "fkv", 1, [("fs", None, 1), ("ft", None, 1)], lambda e, i: e.scalar_tensor_tensor(
            fs[:, :, :], fs[:, :, :], 5.0, ft[:, :, :], ALU.mult, ALU.add))
        once("vector", "fk", 1, [("fkv", None, 1), ("fd", None, 1)], lambda e, i: e.scalar_tensor_tensor(
            ft[:, :, :], fd[:, :, 0:512], 5.0, ft[:, :, :], ALU.mult, ALU.add))

        def turn(name, plane, need, before):
            for c in range(2):
                for j in range(4):
                    once("tensor", name, 1, [(need, None, 1), ("id", None, 1)] + before,
                         lambda e, i, c=c, j=j: e.transpose(
                             pp[6 + c][:, j * HQ:(j + 1) * HQ], plane[:, c, j:512:4], ident[0:HQ, 0:HQ]))

        def turned(c):
            return pp[6 + c][:, 0:4 * HQ].rearrange("p (j r) -> p r j", j=4)

        def place(t, c):
            return t[:, c * 4 * HQ:(c + 1) * 4 * HQ].rearrange("p (r j) -> p r j", j=4)

        def first_nodes():
            for c in range(2):
                once("tensor", "tn0", 1, [("fd", None, 1), ("id", None, 1)], lambda e, i, c=c: e.matmul(
                    pp[7][:, c * HQ:(c + 1) * HQ], fd[:, c, 0:1].broadcast_to([HQ, 128]), ident[0:HQ, 0:HQ],
                    start=True, stop=True))

        once("vector", "n0f", 1, [("tn0", None, 2)], lambda e, i: e.tensor_copy(n0f[:, :], pp[7][:, 0:NQ]))
        once("vector", "n0i", 1, [("n0f", None, 1)], lambda e, i: e.tensor_copy(n0i[:, :], n0f[0:1, :]))
        once("vector", "kbi", 1, [("n0f", None, 1)], lambda e, i: e.tensor_scalar(
            kbi[:, :], n0f[0:1, :], 5.0, None, ALU.mult))

        once("vector", "v1", 1, [("fd", None, 1)], lambda e, i: e.scalar_tensor_tensor(
            junk[:, :, :], fd[:, :, 1:577], 1.0, fd[:, :, 0:576], ALU.mult, ALU.is_lt, accum_out=viol[:, 0:1]))
        once("vector", "v2", 1, [("v1", None, 1)], lambda e, i: e.scalar_tensor_tensor(
            junk[:, :, 0:512], fd[:, :, 64:576], 1.0, fd[:, :, 0:512], ALU.mult, ALU.is_equal,
            accum_out=viol[:, 1:2]))
        once("vector", "v3", 1, [("fd", None, 1)], lambda e, i: e.tensor_tensor(
            viol[:, 2:4], fd[:, :, 511], fd[:, :, 0], ALU.subtract))
        once("vector", "v3r", 1, [("v3", None, 1)], lambda e, i: e.tensor_scalar(
            viol[:, 2:4], viol[:, 2:4], float(SPAN), None, ALU.is_gt))

        for c in range(2):
            once("vector", "reln", 1, [("tn", None, 8), ("n0f", None, 1)], lambda e, i, c=c: e.tensor_tensor(
                place(reln, c), turned(c), n0f[:, c * HQ:(c + 1) * HQ, None].broadcast_to([128, HQ, 4]),
                ALU.subtract))
        for c in range(2):
            once("vector", "kvi", 1, [("tv", None, 8)], lambda e, i, c=c: e.tensor_copy(place(kvi, c), turned(c)))
        for c in range(2):
            once("vector", "keyf", 1, [("tk", None, 8)], lambda e, i, c=c: e.tensor_copy(place(keyf, c), turned(c)))
        once("vector", "t4", 1, [("n0f", None, 1), ("keyf", None, 2)], lambda e, i: e.scalar_tensor_tensor(
            t4[:, :, :], n0f[:, :, None].broadcast_to([128, NQ, 4]), -5.0,
            keyf[:, :].rearrange("p (q j) -> p q j", j=4), ALU.mult, ALU.add))
        once("vector", "pad", 1, [("keyf", None, 2), ("cnt", None, NB)], lambda e, i: e.tensor_scalar(
            cmp1.rearrange("p a b -> p (a b)")[:, 0:NT], keyf[:, :], float(KEYS), -1000.0, ALU.is_ge, ALU.mult))
        once("vector", "relk", 1, [("pad", None, 1), ("t4", None, 1)], lambda e, i: e.tensor_tensor(
            relk[:, :], cmp1.rearrange("p a b -> p (a b)")[:, 0:NT], t4.rearrange("p a b -> p (a b)"), ALU.add))

        def violations():
            once("tensor", "vt", 1, [("v1", None, 1), ("v2", None, 1), ("v3r", None, 1), ("ones", None, 1),
                                     ("keyf", None, 2)],
                 lambda e, i: e.matmul(pp[7][0:1, 256:260], ones[0:HQ, :], viol[:, :], start=True, stop=True))

        once("vector", "tot", 1, [("vt", None, 1)], lambda e, i: e.tensor_copy(tot[0:1, 0:4], pp[7][0:1, 256:260]))
        once("vector", "tot1", 1, [("tot", None, 1)], lambda e, i: e.tensor_scalar(
            tot[0:1, 1:2], tot[0:1, 1:2], 352.0, None, ALU.not_equal))
        once("vector", "v6", 1, [("n0f", None, 1), ("lim6", None, NB)], lambda e, i: e.tensor_tensor(
            v196[0:1, :], n0f[0:1, :], lim6[0:1, :], ALU.is_gt))
        once("vector", "v6r", 1, [("v6", None, 1)], lambda e, i: e.tensor_reduce(
            tot[0:1, 4:5], v196[0:1, :], AX.X, ALU.add))
        for b in range(NB):
            once("vector", "seek", 1, [("rows", None, NB)], lambda e, i, b=b: e.tensor_scalar(
                rowsf[:, b, :], rows[:, b, :], nf[:, b:b + 1], None, ALU.is_lt, op1=ALU.add,
                accum_out=cnt2[:, b:b + 1]))

        once("vector", "stf", 1, [("seek", None, NB), ("cnt1", None, 1)], lambda e, i: e.scalar_tensor_tensor(
            stf[:, :], cnt[:, :], float(SEEK), cnt2[:, :], ALU.mult, ALU.add))
        once("vector", "v4", 1, [("stf", None, 1), ("base", None, 1)], lambda e, i: e.tensor_tensor(
            v25[:, 0, :], stf[:, :], base[:, :], ALU.subtract))
        once("vector", "v5", 1, [("v4", None, 1)], lambda e, i: e.tensor_scalar(
            v25[:, 1, :], v25[:, 0, :], 960.0, None, ALU.is_gt))
        once("vector", "v5b", 1, [("v5", None, 1)], lambda e, i: e.tensor_scalar(
            v25[:, 0, :], v25[:, 0, :], -1024.0, None, ALU.is_lt))
        once("vector", "v5r", 1, [("v5b", None, 1)], lambda e, i: e.tensor_reduce(
            tot[0:1, 5:6], v25[0:1, :, :], AX.XY, ALU.add))
        once("vector", "strel0", 1, [("stf", None, 1), ("base", None, 1)], lambda e, i: e.scalar_tensor_tensor(
            strel[:, 1:NB], stf[:, 1:NB], 1024.0, base[:, 1:NB], ALU.add, ALU.subtract))
        once("vector", "strel", 1, [("strel0", None, 1)], lambda e, i: e.tensor_copy(strel[:, 0:1], stf[:, 0:1]))
        once("vector", "totr", 1, [("v5r", None, 1), ("v6r", None, 1), ("tot1", None, 1)], lambda e, i: e.tensor_reduce(
            tot[0:1, 6:7], tot[0:1, 0:6], AX.X, ALU.add))
        once("vector", "flag", 1, [("totr", None, 1)], lambda e, i: e.tensor_scalar(
            flag[:, :], tot[0:1, 6:7], 0.0, None, ALU.is_gt))

        def lift(e, b, out_, w, r0, r1):
            return e.matmul(out_, xT[:, b * 128:(b + 1) * 128],
                            w[:, r0:r1, :].rearrange("p r c -> p (r c)"), start=True, stop=True)

        def parts(ap):
            return ap.rearrange("p (r c) -> p r c", c=C)

        at = q.at

        def turn_x(b, before):
            P = pp[4 + b % 2][:, 256:384]
            at("tensor", "xt", 1, b, [("xl", None, 2), ("id", None, 1), ("pk2", b - 4), ("xtc", b - 2)],
               lambda e: e.transpose(P, xs[:, b, :], ident[:, :]))
            return lambda: at("scalar", "xtc", 1, b, [("xt", b)] + before, lambda e: e.activation(
                xT[:, b * 128:(b + 1) * 128], P, ACT.Copy))

        def early_q(b, part):
            P = pp[6]
            if part == 0:
                at("tensor", "ea", 1, b, [("wlq", None, 1), ("keyf", None, 2), ("eb", b - 1)],
                   lambda e: lift(e, b, P[:, :], wq, 0, 4))
                at("vector", "eq0", 1, b, [("ea", b), ("el", b - 1)], lambda e: e.tensor_scalar(
                    eqs[:, 0:4, :], parts(P[:, :]), 0.25, None, ALU.mult))
                return
            at("tensor", "ec", 1, b, [("eq0", b)], lambda e: lift(e, b, P[:, 0:C], wq, 4, 5))
            at("vector", "eb", 1, b, [("ec", b), ("el", b - 1)], lambda e: e.tensor_scalar(
                eqs[:, 4, :], P[:, 0:C], 0.25, None, ALU.mult))
            at("vector", "eh", 1, b, [("eb", b), ("tp", b - 1)], lambda e: e.tensor_copy(eqb[:, :, 0, :], eqs[:, :, :]))
            at("vector", "er", 1, b, [("eh", b)], lambda e: e.tensor_tensor(
                eqr[:, :, :], eqs[:, :, :], eqb[:, :, 0, :], ALU.subtract))
            at("vector", "em", 1, b, [("er", b)], lambda e: e.tensor_copy(eqb[:, :, 1, :], eqr[:, :, :]))
            at("vector", "el", 1, b, [("em", b)], lambda e: e.tensor_tensor(
                eqb[:, :, 2, :], eqr[:, :, :], eqb[:, :, 1, :], ALU.subtract))
            at("sync", "tp", (16, 2), b, [("el", b)], lambda e: e.dma_start(
                QF[b * 640:(b + 1) * 640, :].rearrange("(p r) c -> p (r c)", r=R),
                eqb.rearrange("p r m c -> p (r m c)")))

        once("tensor", "wg", 1, [("id", None, 1)],
             lambda e, i: e.transpose(pp[5][:, 0:128], ident[:, :], ident[:, :]))
        q.lists["tensor"].insert(0, q.lists["tensor"].pop())
        turn_x(0, [])()
        turn_x(1, [])()
        for b in range(NB):
            at("tensor", "pa", 1, b, [("xtc", b), ("wl", None, 2), ("pk0", b - 2)],
               lambda e, b=b: lift(e, b, pp[b % 2][:, :], W[:, 0, :, :], 0, 4))
            at("scalar", "pk0", 1, b, [("pa", b), ("tabk", b - 2)], lambda e, b=b: e.activation(
                stg[:, b % 2, 0:4, 0:C], parts(pp[b % 2][:, :]), ACT.Copy))
            at("tensor", "pb", 1, b, [("pk1", b - 2)], lambda e, b=b: lift(e, b, pp[2 + b % 2][:, :], W[:, 1, :, :], 0, 4))
            at("scalar", "pk1", 1, b, [("pb", b), ("tabk", b - 2)], lambda e, b=b: e.activation(
                stg[:, b % 2, 0:4, C:2 * C], parts(pp[2 + b % 2][:, :]), ACT.Copy))
            turned_x = turn_x(b + 2, [("pc", b)]) if b + 2 < NB else None
            at("tensor", "pc", 1, b, [("pk2", b - 2), ("xtc", b)], lambda e, b=b: [
                lift(e, b, pp[4 + b % 2][:, 0:C], W[:, 0, :, :], 4, 5),
                lift(e, b, pp[4 + b % 2][:, C:2 * C], W[:, 1, :, :], 4, 5)][1])
            at("scalar", "pk2", 1, b, [("pc", b), ("tabk", b - 2)], lambda e, b=b: e.activation(
                stg[:, b % 2, 4, :], pp[4 + b % 2][:, 0:2 * C], ACT.Copy))
            if turned_x:
                turned_x()
            at("sync", "tabk", (16, 2), b, [("pk0", b), ("pk1", b), ("pk2", b)], lambda e, b=b: e.dma_start(
                KV[b * 640:(b + 1) * 640, :].rearrange("(p r) c -> p (r c)", r=R),
                stg[:, b % 2, :, :].rearrange("p r c -> p (r c)")))
            if b == 1:
                first_nodes()
            if b in EARLY:
                early_q(EARLY.index(b) // 2, EARLY.index(b) % 2)
            if b == TURNS[0]:
                turn("tn", fd, "fd", [("cmp", None, 1), ("n0f", None, 1)])
            elif b == TURNS[1]:
                turn("tv", fs, "fkv", [("reln", None, 2)])
            elif b == TURNS[2]:
                turn("tk", ft, "fk", [("kvi", None, 2)])
            elif b == TURNS[3]:
                violations()
            elif b == TURNS[4]:
                once("tensor", "pfree", 1, [("wlo", None, 5), ("tot", None, 1)],
                     lambda e, i: e.transpose(pp[7][:, 0:128], woS[:, :], ident[:, :]))
        once("vector", "woT", 1, [("pfree", None, 1)], lambda e, i: e.tensor_copy(woT[:, :], pp[7][:, 0:128]))

        slow = Queues(nc, ctx, q)
        for s in range(2):
            slow.once("vector", "stb", 1, [("wlo", None, 5)],
                      lambda e, i, s=s: e.tensor_copy(stq[:, s, :, C:QW], bb[:, :, :]))
        slow.loop(NB, [
            ("tensor", "pd", 1, [("wlq", None, 1), ("pk0", None, NB), ("pk1", None, NB), ("pk2", None, NB), ("pq0", -2)],
             lambda e, b: lift(e, b, pp[b % 2][:, :], wq, 0, 4)),
            ("scalar", "pq0", 1, [("pd", 0), ("tabq", -2)], lambda e, b: e.activation(
                stq[:, b % 2, 0:4, 0:C], parts(pp[b % 2][:, :]), ACT.Copy, scale=0.25)),
            ("tensor", "pe", 1, [("pq1", -2)], lambda e, b: lift(e, b, pp[2 + b % 2][:, 0:C], wq, 4, 5)),
            ("vector", "pq1", 1, [("pe", 0), ("tabq", -2)], lambda e, b: e.tensor_scalar(
                stq[:, b % 2, 4, 0:C], pp[2 + b % 2][:, 0:C], 0.25, None, ALU.mult)),
            ("sync", "tabq", (16, 2), [("pq0", 0), ("pq1", 0), ("stb", None, 2)], lambda e, b: e.dma_start(
                QT[b * 640:(b + 1) * 640, :].rearrange("(p r) c -> p (r c)", r=R),
                stq[:, b % 2, :, :].rearrange("p r c -> p (r c)"))),
        ], False)
        general(slow, pp, locals())
        finish(slow, pp, locals())
        quick = Queues(nc, ctx, q)
        fast(quick, pp, locals())

        for one in (q, slow, quick):
            one.number()
        block = ctx.enter_context(nc.Block())

        def run(key, e):
            q.emit(key, e)
            q.steps["flag"].wait(e, 0)
            reg = e.alloc_register("way")
            e.reg_load(reg, flag[0:1, 0:1])
            way = e.snap(reg, min_val=0, max_val=1)
            with e.If(way):
                slow.emit(key, e)
                if key == "sync":
                    for name, n in (("mx0", 1), ("acc0", 1), ("gsm", NT), ("gsa", NT), ("outd", 2),
                                    ("tabq", NB)):
                        slow.steps[name].wait_all(e, n)
            with e.Else():
                quick.emit(key, e)
                if key == "sync":
                    for name, n in quick.ends:
                        quick.steps[name].wait_all(e, n)
            if key == "sync":
                q.steps["tabk"].wait_all(e, NB)

        @block.sync
        def _(e):
            run("sync", e)

        @block.scalar
        def _(e):
            run("scalar", e)

        @block.vector
        def _(e):
            run("vector", e)

        @block.gpsimd
        def _(e):
            run("gpsimd", e)

        @block.tensor
        def _(e):
            run("tensor", e)


def general(q, pp, v):
    once, loop = q.once, q.loop
    KV, QT, MX, ACC = v["KV"], v["QT"], v["MX"], v["ACC"]
    keyf, kvi, ident, pid, aggT = (v[k] for k in ("keyf", "kvi", "ident", "pid", "aggT"))
    room = Region(v["ring"][:, :])

    def sb(name, shape, dt=F32):
        return room.take(shape[1:], dt)

    keyi = sb("g_keyi", [128, NT], U32)
    tri = sb("g_tri", [128, 128])
    once("gpsimd", "tri0", 1, [("flag", None, 1)], lambda e, i: e.memset(tri[:, :], 1.0))
    once("gpsimd", "tri", 1, [("tri0", None, 1)], lambda e, i: e.affine_select(
        out=tri[:, :], in_=tri[:, :], compare_op=ALU.is_gt, fill=0.0, base=0,
        pattern=[[-1, 128]], channel_multiplier=1))
    once("vector", "keyi", 1, [], lambda e, i: e.tensor_copy(keyi[:, :], keyf[:, :]))
    fillm = sb("fillm", [128, H])
    filla = sb("filla", [128, AW])
    kc = sb("g_kc", [128, 1])
    ki = sb("g_ki", [128, 1], U32)
    vi = sb("g_vi", [128, 1], U32)
    gkv = sb("g_kv", [128, 2 * C])
    gq = sb("g_q", [128, QW])
    gm = sb("g_m", [128, H])
    ga = sb("g_a", [128, AW])
    prod = sb("g_prod", [128, C])
    lg = sb("g_lg", [128, H])
    L = sb("g_L", [128, NT * H])
    ne = sb("g_ne", [128, 128])
    eq = sb("g_eq", [128, 128])
    tmp = sb("g_tmp", [128, 128])
    dup = sb("g_dup", [128, 1])
    dfar = sb("g_dfar", [128, 1])
    wf = sb("g_wf", [128, 1])
    wi = sb("g_wi", [128, 1], U32)
    widx = sb("g_widx", [128, NT], U32)
    X = sb("g_X", [128, H, 128])
    mx = sb("g_mx", [128, H])
    ex = sb("g_ex", [128, H])
    EV = sb("g_EV", [128, AW])
    up = sb("g_up", [128, AW])
    KR, LB0, LB1, TT = pp[0][:, 0:128], pp[1], pp[2], pp[3][:, 0:AW]
    at = bass.ds

    def gather(buf, tab, idx):
        return lambda e, i: e.indirect_dma_start(buf[:, :], None, tab, bass.IndirectOffsetOnAxis(idx[:, 0:1], 0))

    def scatter(buf, tab, idx):
        return lambda e, i: e.indirect_dma_start(tab, bass.IndirectOffsetOnAxis(idx[:, 0:1], 0), buf[:, :], None)

    def row_of(col):
        return lambda e, i: e.matmul(KR, col[:, 0:1].broadcast_to([128, 128]), ident[:, :], start=True, stop=True)

    def spread(e, i):
        for h in range(H):
            last = e.matmul((LB0, LB1)[h // 4][:, (h % 4) * 128:(h % 4 + 1) * 128],
                            lg[:, h:h + 1].broadcast_to([128, 128]), ident[:, :], start=True, stop=True)
        return last

    once("vector", "fm", 1, [], lambda e, i: e.memset(fillm[:, :], NEG))
    once("vector", "fa", 1, [], lambda e, i: e.memset(filla[:, :], 0.0))
    once("sync", "mx0", 16, [("fm", None, 1)], lambda e, i: e.dma_start(
        MX.rearrange("(p r) c -> p r c", p=128), fillm[:, None, :].broadcast_to([128, ROWS // 128, H])))
    once("sync", "acc0", 16, [("fa", None, 1)], lambda e, i: e.dma_start(
        ACC.rearrange("(p r) c -> p r c", p=128), filla[:, None, :].broadcast_to([128, ROWS // 128, AW])))
    once("vector", "dfar", 1, [("pid", None, 1)], lambda e, i: e.tensor_scalar(
        dfar[:, :], pid[:, :], float(DUP_ROW), None, ALU.add))

    loop(NT, [
        ("vector", "akc", 1, [("adup", -1), ("awf", -1), ("akr", -1)],
         lambda e, i: e.tensor_copy(kc[:, :], keyf[:, at(i, 1)])),
        ("vector", "aki", 1, [("keyi", None, 1), ("agq", -1), ("agm", -1)],
         lambda e, i: e.tensor_copy(ki[:, :], keyi[:, at(i, 1)])),
        ("vector", "avi", 1, [("agk", -1)],
         lambda e, i: e.tensor_copy(vi[:, :], kvi[:, at(i, 1)])),
        ("gpsimd", "agk", 16, [("avi", 0), ("tabk", None, NB), ("aprod", -1)], gather(gkv, KV, vi)),
        ("gpsimd", "agq", 16, [("aki", 0), ("tabq", None, NB), ("alg", -1)], gather(gq, QT, ki)),
        ("gpsimd", "agm", 16, [("aki", 0), ("mx0", None, 1), ("gsm", -1), ("amx2", -1)], gather(gm, MX, ki)),
        ("tensor", "akr", 1, [("akc", 0), ("id", None, 1), ("aeq", -1), ("pq0", None, NB)], row_of(kc)),
        ("vector", "ane", 1, [("akr", 0), ("akc", 0), ("aX0", -1), ("aX1", -1)], lambda e, i: e.tensor_scalar(
            ne[:, :], KR, kc[:, 0:1], FAR, ALU.not_equal, ALU.mult)),
        ("vector", "aeq", 1, [("akr", 0), ("akc", 0), ("adup", -1)], lambda e, i: e.tensor_scalar(
            eq[:, :], KR, kc[:, 0:1], None, ALU.is_equal)),
        ("vector", "atmp", 1, [("aeq", 0), ("tri", None, 1), ("adup", -1)], lambda e, i: e.tensor_tensor(
            tmp[:, :], eq[:, :], tri[:, :], ALU.mult)),
        ("vector", "adup", 1, [("atmp", 0), ("awf", -1)], lambda e, i: e.tensor_reduce(
            dup[:, :], tmp[:, :], AX.X, ALU.add)),
        ("vector", "adup1", 1, [("adup", 0)], lambda e, i: e.tensor_scalar(
            dup[:, :], dup[:, :], 0.0, None, ALU.is_gt)),
        ("vector", "awf0", 1, [("akc", 0), ("dfar", None, 1), ("awi", -1)], lambda e, i: e.tensor_tensor(
            wf[:, :], dfar[:, :], kc[:, :], ALU.subtract)),
        ("vector", "awf1", 1, [("awf0", 0), ("adup1", 0)], lambda e, i: e.tensor_tensor(
            wf[:, :], wf[:, :], dup[:, :], ALU.mult)),
        ("vector", "awf", 1, [("awf1", 0)], lambda e, i: e.tensor_tensor(
            wf[:, :], wf[:, :], kc[:, :], ALU.add)),
        ("vector", "awi", 1, [("awf", 0), ("gsm", -1)], lambda e, i: e.tensor_copy(wi[:, :], wf[:, :])),
        ("vector", "awx", 1, [("awf", 0)], lambda e, i: e.tensor_copy(widx[:, at(i, 1)], wf[:, :])),
        ("vector", "aprod", 1, [("agk", 0), ("agq", 0), ("alg0", -1)], lambda e, i: e.tensor_tensor(
            prod[:, :], gkv[:, 0:C], gq[:, 0:C], ALU.mult)),
        ("vector", "alg0", 1, [("aprod", 0), ("abc", -1)], lambda e, i: e.tensor_reduce(
            lg[:, :], prod[:, :].rearrange("p (h d) -> p h d", d=D), AX.X, ALU.add)),
        ("vector", "alg", 1, [("alg0", 0), ("agq", 0)], lambda e, i: e.tensor_tensor(
            lg[:, :], lg[:, :], gq[:, C:QW], ALU.add)),
        ("vector", "aL", 1, [("alg", 0)], lambda e, i: e.tensor_copy(L[:, at(i * H, H)], lg[:, :])),
        ("tensor", "abc", 1, [("alg", 0), ("aX0", -1), ("aX1", -1), ("pk1", None, NB)], spread),
        ("vector", "aX0", 1, [("abc", 0), ("ane", 0), ("amx", -1)], lambda e, i: e.tensor_tensor(
            X[:, 0:4, :], LB0[:, :].rearrange("p (h j) -> p h j", h=4),
            ne[:, None, :].broadcast_to([128, 4, 128]), ALU.add)),
        ("vector", "aX1", 1, [("abc", 0), ("ane", 0), ("amx", -1)], lambda e, i: e.tensor_tensor(
            X[:, 4:8, :], LB1[:, :].rearrange("p (h j) -> p h j", h=4),
            ne[:, None, :].broadcast_to([128, 4, 128]), ALU.add)),
        ("vector", "amx", 1, [("aX0", 0), ("aX1", 0), ("gsm", -1)], lambda e, i: e.tensor_reduce(
            mx[:, :], X[:, :, :], AX.X, ALU.max)),
        ("vector", "amx2", 1, [("amx", 0), ("agm", 0)], lambda e, i: e.tensor_tensor(
            mx[:, :], mx[:, :], gm[:, :], ALU.max)),
        ("gpsimd", "gsm", 16, [("amx2", 0), ("awi", 0), ("agm", 0)], scatter(mx, MX, wi)),
    ], True)

    loop(NT, [
        ("vector", "bkc", 1, [("beq", -1), ("bkr", -1), ("gsm", None, NT), ("akr", None, NT), ("abc", None, NT)],
         lambda e, i: e.tensor_copy(kc[:, :], keyf[:, at(i, 1)])),
        ("vector", "bki", 1, [("bgm", -1), ("bga", -1)],
         lambda e, i: e.tensor_copy(ki[:, :], keyi[:, at(i, 1)])),
        ("vector", "bvi", 1, [("bgk", -1)], lambda e, i: e.tensor_copy(vi[:, :], kvi[:, at(i, 1)])),
        ("vector", "bwi", 1, [("gsa", -1), ("awx", None, NT)],
         lambda e, i: e.tensor_copy(wi[:, :], widx[:, at(i, 1)])),
        ("gpsimd", "bgk", 16, [("bvi", 0), ("bev", -1)], gather(gkv, KV, vi)),
        ("gpsimd", "bgm", 16, [("bki", 0), ("bsub", -1)], gather(gm, MX, ki)),
        ("gpsimd", "bga", 16, [("bki", 0), ("acc0", None, 1), ("gsa", -1), ("bup", -1)], gather(ga, ACC, ki)),
        ("tensor", "bkr", 1, [("bkc", 0), ("beq", -1)], row_of(kc)),
        ("vector", "beq", 1, [("bkr", 0), ("bkc", 0), ("btt", -1)], lambda e, i: e.tensor_scalar(
            eq[:, :], KR, kc[:, 0:1], None, ALU.is_equal)),
        ("vector", "bsub", 1, [("bgm", 0), ("bexp", -1), ("aL", None, NT)], lambda e, i: e.tensor_tensor(
            ex[:, :], L[:, at(i * H, H)], gm[:, :], ALU.subtract)),
        ("scalar", "bexp", 1, [("bsub", 0), ("btt", -1)], lambda e, i: e.activation(
            EV[:, C:AW], ex[:, :], ACT.Exp)),
        ("vector", "bev", 1, [("bexp", 0), ("bgk", 0), ("btt", -1)], lambda e, i: e.tensor_tensor(
            EV[:, 0:C].rearrange("p (h d) -> p h d", d=D), gkv[:, C:2 * C].rearrange("p (h d) -> p h d", d=D),
            EV[:, C:AW, None].broadcast_to([128, H, D]), ALU.mult)),
        ("tensor", "btt", 1, [("bev", 0), ("beq", 0), ("bup", -1)], lambda e, i: e.matmul(
            TT, eq[:, :], EV[:, :], start=True, stop=True)),
        ("vector", "bup", 1, [("btt", 0), ("bga", 0), ("gsa", -1)], lambda e, i: e.tensor_tensor(
            up[:, :], ga[:, :], TT, ALU.add)),
        ("gpsimd", "gsa", 16, [("bup", 0), ("bwi", 0), ("bga", 0)], scatter(up, ACC, wi)),
    ], True)

    ca = sb("c_a", [128, R, AW])
    cs = sb("c_s", [128, R, H])
    cg = sb("c_g", [128, C])
    loop(NB, [
        ("sync", "cld", 16, [("gsa", None, NT), ("cmul", -1)], lambda e, b: e.dma_start(
            ca[:, :, :].rearrange("p r c -> p (r c)"),
            ACC[b * 640:(b + 1) * 640, :].rearrange("(p r) c -> p (r c)", r=R))),
        ("vector", "ceps", 1, [("cld", 0), ("cmul", -1)], lambda e, b: e.tensor_scalar(
            cs[:, :, :], ca[:, :, C:AW], 1e-12, None, ALU.add)),
        ("vector", "crec", 1, [("ceps", 0)], lambda e, b: e.reciprocal(cs[:, :, :], cs[:, :, :])),
    ] + [
        ("vector", f"cm{r}", 1, [("crec", 0)], lambda e, b, r=r: e.tensor_tensor(
            ca[:, r, 0:C].rearrange("p (h d) -> p h d", d=D), ca[:, r, 0:C].rearrange("p (h d) -> p h d", d=D),
            cs[:, r, :, None].broadcast_to([128, H, D]), ALU.mult)) for r in range(R)
    ] + [
        ("vector", "cmul", 1, [(f"cm{r}", 0) for r in range(R)] + [("ctr", -1)], lambda e, b: e.tensor_reduce(
            cg[:, :], ca[:, :, 0:C].rearrange("p r c -> p c r"), AX.X, ALU.add)),
        ("tensor", "ctr", 1, [("cmul", 0), ("agg", -1)], lambda e, b: e.transpose(
            pp[4][:, 0:128], cg[:, :], ident[:, :])),
        ("vector", "agg", 1, [("ctr", 0)], lambda e, b: e.tensor_copy(
            aggT[:, b * 128:(b + 1) * 128], pp[4][:, 0:128])),
    ], False)


def finish(q, pp, v):
    loop = q.loop
    xs, aggT, woT, bob, gab, beb, out = (v[k] for k in ("xs", "aggT", "woT", "bob", "gab", "beb", "out"))
    room = Region(v["pool"][:, :])
    res = room.take([NB, C])
    hb = room.take([2, C])
    st = room.take([2, 6])
    mv = room.take([2, 2])
    sd = room.take([2])
    epst = room.take([1])
    q.once("vector", "feps", 1, [], lambda e, i: e.memset(epst[:, :], EPS))

    def stats(p, src, before):
        return [
            ("vector", f"{p}bs", 1, before, lambda e, b: e.bn_stats(st[:, b % 2, :], src(b))),
            ("vector", f"{p}ba", 1, [(f"{p}bs", 0)], lambda e, b: e.bn_aggr(mv[:, b % 2, :], st[:, b % 2, :])),
            ("scalar", f"{p}sq", 1, [(f"{p}ba", 0), ("feps", None, 1)], lambda e, b: e.activation(
                sd[:, b % 2:b % 2 + 1], mv[:, b % 2, 1:2], ACT.Sqrt, bias=epst[:, 0:1])),
            ("vector", f"{p}rc", 1, [(f"{p}sq", 0)], lambda e, b: e.reciprocal(
                sd[:, b % 2:b % 2 + 1], sd[:, b % 2:b % 2 + 1])),
            ("vector", f"{p}nm", 1, [(f"{p}rc", 0)], lambda e, b: e.tensor_scalar(
                src(b), src(b), mv[:, b % 2, 0:1], sd[:, b % 2:b % 2 + 1], ALU.subtract, ALU.mult)),
        ]

    h = lambda b: hb[:, b % 2, :]
    body = [
        ("tensor", "fo", 1, [("agg", None, NB), ("fh0", -1)], lambda e, b: e.matmul(
            pp[6][:, 0:128], aggT[:, b * 128:(b + 1) * 128], woT[:, :], start=True, stop=True)),
        ("vector", "fh0", 1, [("fo", 0), ("fcp", -1)], lambda e, b: e.tensor_tensor(h(b), pp[6][:, 0:128], bob[:, :], ALU.add)),
        ("vector", "fh1", 1, [("fh0", 0)], lambda e, b: e.tensor_tensor(h(b), h(b), xs[:, b, :], ALU.add)),
    ] + stats("f", h, [("fh1", 0)]) + [
        ("vector", "fg", 1, [("fnm", 0)], lambda e, b: e.tensor_tensor(h(b), h(b), gab[:, :], ALU.mult)),
        ("vector", "fb", 1, [("fg", 0)], lambda e, b: e.tensor_tensor(h(b), h(b), beb[:, :], ALU.add)),
        ("vector", "fx", 1, [("fb", 0)], lambda e, b: e.tensor_tensor(h(b), h(b), xs[:, b, :], ALU.add)),
    ] + stats("g", h, [("fx", 0)]) + [
        ("vector", "fcp", 1, [("gnm", 0), ("tabq", None, NB)], lambda e, b: e.tensor_copy(res[:, b, :], h(b))),
    ]
    loop(NB, body, False)
    q.once("sync", "outd", 16, [("fcp", None, NB)], lambda e, i: e.dma_start(
        out[0:3072, :].rearrange("(b p) c -> p b c", p=128), res[:, 0:24, :]))
    q.once("sync", "outd", 16, [("fcp", None, NB)], lambda e, i: e.dma_start(out[3072:N, :], res[0:53, 24, :]))


def fast(q, pp, v):
    q.ends = []
    at = q.at
    ring, xs, aggT, hb, keyf, kvi, relk, reln = (
        v[k] for k in ("ring", "xs", "aggT", "hb", "keyf", "kvi", "relk", "reln"))
    woT, bb, bob, gab, beb, identb, nk, io32, strel, n0i, kbi = (
        v[k] for k in ("woT", "bb", "bob", "gab", "beb", "identb", "nk", "io32", "strel", "n0i", "kbi"))
    wq, ident = v["wq"], v["ident"]
    negb = v["negb"]
    pid, KV, QF, CT, LB, out = (v[k] for k in ("pid", "KV", "QF", "CT", "LB", "out"))
    kv = ring[:, :].rearrange("p (s j c) -> p s j c", s=KR, j=4)
    room = Region(v["pool"][:, :])
    ohr = room.take([OR, 4 * C], BF16)
    ab = room.take([4 * C], BF16)
    X = room.take([2, H, SLOTS])
    prod = room.take([4 * C])
    av = room.take([2, 4 * C])
    xqT = room.take([C])
    stq = room.take([R, 3, C], BF16)
    assert room.off <= POOL
    sb = v["sb"]
    qwin = sb("qwin", [128, 2, 3 * C], BF16)
    cwin = sb("cwin", [128, 3, 48], BF16)
    ohn = sb("ohn", [128, 2, 4, 32])
    LR = sb("LR", [128, KR, 4, LC])
    lwin = sb("lwin", [128, SLOTS * LC])
    pen = sb("pen", [128, 2, SLOTS])
    mxs = sb("mxs", [128, R, H])
    m2 = sb("m2", [128, R, H])
    sm = sb("sm", [128, R, H])
    c16 = sb("c16", [128, R, 16])
    cres = sb("cres", [128, R, 16])
    cst = sb("cst", [128, R, 3, 16], BF16)
    tt = sb("tt", [128, 2, 4, H])
    te = sb("te", [128, 2, 4, H])
    npid = sb("npid", [128, 1])
    one = sb("one", [128, 1])
    epst = sb("epst", [128, 1])
    st = sb("st", [128, 2, 6])
    mv = sb("mv", [128, 2, 10, 2])
    sd = sb("sd", [128, 2, 10])

    at("vector", "npid", 1, 0, [("pid", None, 1)], lambda e: e.tensor_scalar(
        npid[:, :], pid[:, :], -1.0, None, ALU.mult))
    at("vector", "one", 1, 0, [], lambda e: e.memset(one[:, :], 1.0))
    at("vector", "eps", 1, 0, [], lambda e: e.memset(epst[:, :], EPS))
    at("vector", "az", 1, 0, [], lambda e: e.memset(aggT[:, :], 0.0))

    regs = {}

    def values(e, key, table, what, k):
        if k % 8 == 0 or (key, what) not in regs:
            base = k - k % 8
            n = min(8, NQ - base)
            if (key, what) not in regs:
                regs[key, what] = [e.alloc_register(f"{what}{m}") for m in range(8)]
            e.load(regs[key, what][:n], table[0:1, base:base + n])
        top = (N - 1) * (5 if table is kbi else 1)
        return e.snap(regs[key, what][k % 8], min_val=0, max_val=top)

    def gathers(k):
        def emit(e):
            return [e.indirect_dma_start(
                kv[:, k % KR, j, :], None, KV, bass.IndirectOffsetOnAxis(kvi[:, 4 * k + j:4 * k + j + 1], 0))
                for j in range(4)]
        at("gpsimd", "kv", (16, 6, 4), k, [("tabk", None, NB), ("woT", None, 1), ("av", k - KR), ("prod", k - KR), ("kv", k - 6)]
           , emit)

    def spread(k):
        def emit(e):
            for j in range(4):
                last = e.matmul(pp[0][:, j * C:(j + 1) * C],
                                relk[:, 4 * k + j:4 * k + j + 1].broadcast_to([128, 128]), identb[:, :],
                                start=True, stop=True)
            return last
        at("tensor", "bc", 1, k, [("relk", None, 1), ("idb", None, 1), ("pk0", None, NB), ("abs", k - 1)], emit)
        at("scalar", "abs", 1, k, [("bc", k), ("npid", 0), ("oh", k - 1), ("tabk", None, NB)],
           lambda e: e.activation(ab[:, :], pp[0][:, :], ACT.Abs, bias=npid[:, 0:1]))
        at("scalar", "oh", 1, k, [("abs", k), ("one", 0), ("ce", k - OR)],
           lambda e: e.activation(ohr[:, k % OR, :], ab[:, :], ACT.Relu, bias=one[:, 0:1], scale=-1.0))

    def load_q(k):
        at("sync", "qw", (16, 3), k, [("tp", None, 2), ("tq", max(last_block(k) - 2, -1)), ("kbi", None, 1), ("qe", k - 2)],
           lambda e: e.dma_start(qwin[:, k % 2, :], QF[bass.ds(values(e, "sync", kbi, "kq", k), 128), :]))

    def make_q(b, turn):
        n = b - 2
        if turn == 0:
            at("tensor", "xq", 1, n, [("pk1", None, NB), ("ql1", n - 1)],
               lambda e: e.transpose(pp[1][:, 0:C], xs[:, b, :], ident[:, :]))
            at("scalar", "xqc", 1, n, [("xq", n), ("qa1", n - 1), ("tabk", None, NB)],
               lambda e: e.activation(xqT[:, :], pp[1][:, 0:C], ACT.Copy, scale=0.25))
            return
        half, part = divmod(turn - 1, 3)
        r0, r1 = (0, 4) if half == 0 else (4, R)
        P = pp[1][:, 0:(r1 - r0) * C]
        sums, cut = (("qa", "qh"), ("qs", "qm"), ("qt", "ql"))[part]

        def emit(e):
            last = e.matmul(P, xqT[:, :], wq[:, r0:r1, :].rearrange("p r c -> p (r c)"), start=True, stop=part == 0)
            for m in range(part):
                last = e.matmul(P.rearrange("p (r c) -> p r c", c=C), negb[:, :], stq[:, r0:r1, m, :],
                                start=False, stop=m == part - 1)
            return last
        before = ("xqc", n) if turn == 1 else (("qh0", "qm0", "ql0", "qh1", "qm1")[turn - 2], n)
        at("tensor", f"{sums}{half}", 1, n, [before, ("wlq", None, 1), ("idn", None, 1)], emit)
        at("scalar", f"{cut}{half}", 1, n, [(f"{sums}{half}", n), ("tq", n - 1)], lambda e: e.activation(
            stq[:, r0:r1, part, :], P.rearrange("p (r c) -> p r c", c=C), ACT.Copy))
        if turn == 6:
            at("sync", "tq", (16, 2), n, [("ql1", n)], lambda e: e.dma_start(
                QF[b * 640:(b + 1) * 640, :].rearrange("(p r) c -> p (r c)", r=R),
                stq[:, :, :, :].rearrange("p r m c -> p (r m c)")))

    def queries(k):
        def emit(e):
            for j in range(4):
                for m in range(3):
                    last = e.matmul(pp[2 + k % 2][:, j * C:(j + 1) * C], ohr[:, k % OR, j * C:(j + 1) * C],
                                    qwin[:, k % 2, m * C:(m + 1) * C], start=(m == 0), stop=(m == 2))
            return last
        at("tensor", "qe", 1, k, [("oh", k), ("qw", k), ("prod", k - 2)], emit)

    def holders(k):
        return [b for b in range(NB) if first_quad(b) <= k <= last_quad(b)]

    written = {}

    def logits(k, part):
        used = [(f"lb{b}", None, last_quad(b) - first_quad(b) + 1) for b in holders(k - KR)] if k >= KR else []
        if part == 0:
            at("vector", "prod", 1, k, [("qe", k), ("kv", k), ("red", k - 1)], lambda e: e.tensor_tensor(
                prod[:, :].rearrange("p (j c) -> p j c", j=4), pp[2 + k % 2][:, :].rearrange("p (j c) -> p j c", j=4),
                kv[:, k % KR, :, 0:C], ALU.mult))
        elif part == 1:
            at("vector", "red", 1, k, [("prod", k), ("ta", k - KR)] + used, lambda e: e.tensor_reduce(
                LR[:, k % KR, :, 0:H], prod[:, :].rearrange("p (j h d) -> p j h d", j=4, d=D), AX.X, ALU.add))
        elif part == 2:
            at("vector", "kc", 1, k, [("keyf", None, 2)] + used, lambda e: e.tensor_copy(
                LR[:, k % KR, :, H], keyf[:, 4 * k:4 * k + 4]))
        else:
            for b in holders(k):
                t = written.get(b, 0)
                written[b] = t + 1
                f = (k - first_quad(b)) * 512
                at("sync", f"lb{b}", 16, t, [("red", k), ("kc", k)], lambda e, b=b, f=f: e.dma_start(
                    LB[b][f:f + 512, :].rearrange("(p j) c -> p (j c)", j=4),
                    LR[:, k % KR, :, :].rearrange("p j c -> p (j c)")))

    def fetch(b):
        n = last_quad(b) - first_quad(b) + 1
        at("gpsimd", "sg", (16, 2), b, [(f"lb{b}", None, n), ("xa", R * b - 1)],
           lambda e: e.indirect_dma_start(lwin[:, :], None, LB[b], bass.IndirectOffsetOnAxis(strel[:, b:b + 1], 0)))

    def maxima(t, part):
        b, r = divmod(t, R)
        win = lwin.rearrange("p (j c) -> p c j", c=LC)
        if part == 0:
            at("vector", "pen", 1, t, [("sg", b), ("xa", t - 2), ("nk", None, 1)], lambda e: e.tensor_scalar(
                pen[:, t % 2, :], win[:, H, :], nk[:, r, b:b + 1], FAR, ALU.not_equal, ALU.mult))
        elif part == 1:
            at("vector", "xa", 1, t, [("pen", t), ("ex", t - 2)], lambda e: e.tensor_tensor(
                X[:, t % 2, :, :], win[:, 0:H, :], pen[:, t % 2, None, :].broadcast_to([128, H, SLOTS]), ALU.add))
        elif part == 2:
            at("vector", "xm", 1, t, [("xa", t), ("ms", t - R)], lambda e: e.tensor_reduce(
                mxs[:, r, :], X[:, t % 2, :, :], AX.X, ALU.max))
        elif part == 3:
            at("vector", "ms", 1, t, [("xm", t), ("mt", t - R)], lambda e: e.tensor_tensor(
                m2[:, r, :], mxs[:, r, :], bb[:, r, :], ALU.add))
        else:
            at("vector", "mt", 1, t, [("ms", t), ("ex", t - R), ("cl1", b - 1)],
               lambda e: e.scalar_tensor_tensor(
                   c16[:, r, 0:H], m2[:, r, :], NEG, bb[:, r, :], ALU.max, ALU.subtract, reverse1=True))

    def exps(t):
        b, r = divmod(t, R)

        def emit(e):
            return [e.activation(X[:, t % 2, h, :], X[:, t % 2, h, :], ACT.Exp, bias=c16[:, r, h:h + 1],
                                 accum_out=sm[:, r, h:h + 1]) for h in range(H)]
        at("scalar", "ex", (1, 1, H), t, [("mt", t), ("ra", b - 1)], emit)

    def constants(b):
        at("vector", "ra", 1, b, [("ex", R * b + R - 1)], lambda e: e.tensor_scalar(
            c16[:, :, H:16], sm[:, :, :], 1e-12, None, ALU.add))
        at("vector", "rb", 1, b, [("ra", b)], lambda e: e.reciprocal(c16[:, :, H:16], c16[:, :, H:16]))
        cs = cst[:, :, :, :]
        at("vector", "ch", 1, b, [("rb", b), ("cw", b - 1)], lambda e: e.tensor_copy(cs[:, :, 0, :], c16[:, :, :]))
        at("vector", "cl0", 1, b, [("ch", b)], lambda e: e.tensor_tensor(
            cres[:, :, :], c16[:, :, :], cs[:, :, 0, :], ALU.subtract))
        at("vector", "cm", 1, b, [("cl0", b)], lambda e: e.tensor_copy(cs[:, :, 1, :], cres[:, :, :]))
        at("vector", "cl1", 1, b, [("cm", b)], lambda e: e.tensor_tensor(
            cs[:, :, 2, :], cres[:, :, :], cs[:, :, 1, :], ALU.subtract))
        at("sync", "cw", (16, 2), b, [("cl1", b)], lambda e: e.dma_start(
            CT[b * 640:(b + 1) * 640, :].rearrange("(p r) c -> p (r c)", r=R),
            cs.rearrange("p r m c -> p (r m c)")))

    def load_c(k):
        n = last_block(k) + 1
        at("sync", "cl", (16, 3), k, [("cw", None, n), ("kbi", None, 1), ("ce", k - 3)],
           lambda e: e.dma_start(cwin[:, k % 3, :], CT[bass.ds(values(e, "sync", kbi, "kc", k), 128), :]))

    def bring(k):
        def emit(e):
            for j in range(4):
                for m in range(3):
                    last = e.matmul(pp[4 + k % 2][:, j * 16:(j + 1) * 16], ohr[:, k % OR, j * C:(j + 1) * C],
                                    cwin[:, k % 3, m * 16:(m + 1) * 16], start=(m == 0), stop=(m == 2))
            return last
        at("tensor", "ce", 1, k, [("oh", k), ("cl", k), ("atn", k - 2)], emit)

    def consts_of(k, lo):
        return pp[4 + k % 2][:, 0:64].rearrange("p (j c) -> p j c", j=4)[:, :, lo:lo + H]

    def shift(k):
        at("vector", "ta", 1, k, [("ce", k), ("te", k - 2), ("red", k)], lambda e: e.tensor_tensor(
            tt[:, k % 2, :, :], LR[:, k % KR, :, 0:H], consts_of(k, 0), ALU.add))
        at("scalar", "te", 1, k, [("ta", k), ("atn", k - 2)], lambda e: e.activation(
            te[:, k % 2, :, :], tt[:, k % 2, :, :], ACT.Exp))

    def weigh(k, part):
        if part == 0:
            at("vector", "on", 1, k, [("reln", None, 2), ("io32", None, 1), ("ag", k - 2)], lambda e: e.tensor_tensor(
                ohn[:, k % 2, :, :], reln[:, 4 * k:4 * k + 4, None].broadcast_to([128, 4, 32]),
                io32[:, None, :].broadcast_to([128, 4, 32]), ALU.is_equal))
        elif part == 1:
            at("vector", "atn", 1, k, [("te", k), ("av", k - 2)], lambda e: e.tensor_tensor(
                te[:, k % 2, :, :], te[:, k % 2, :, :], consts_of(k, H), ALU.mult))
        else:
            at("vector", "av", 1, k, [("atn", k), ("ag", k - 2)], lambda e: e.tensor_tensor(
                av[:, k % 2, :].rearrange("p (j h d) -> p j h d", j=4, d=D),
                kv[:, k % KR, :, C:2 * C].rearrange("p j (h d) -> p j h d", d=D),
                te[:, k % 2, :, :, None].broadcast_to([128, 4, H, D]), ALU.mult))

    def collect(k):
        def emit(e):
            for j in range(4):
                last = e.matmul(pp[6 + k % 2][:, 0:32], av[:, k % 2, j * C:(j + 1) * C], ohn[:, k % 2, j, :],
                                start=(j == 0), stop=(j == 3))
            return last
        at("tensor", "ag", 1, k, [("av", k), ("on", k), ("aa", k - 2)]
           + [("h0", b) for b in range(NB) if last_quad(b) + 1 == k - 2], emit)

    def gather_in(k):
        def emit(e):
            to = aggT[:, bass.ds(values(e, "vector", n0i, "na", k), 32)]
            return e.tensor_tensor(to, to, pp[6 + k % 2][:, 0:32], ALU.add)
        at("vector", "aa", 1, k, [("ag", k), ("az", 0), ("aa", k - 1), ("n0i", None, 1)], emit)

    groups = (range(0, 5), range(5, 10), range(10, 15), range(15, 20), range(20, 23), range(23, NB))
    group = {b: g for g, members in enumerate(groups) for b in members}

    def span(g):
        return groups[g][0] % 10, groups[g][-1] % 10 + 1

    def project(b):
        P = pp[6 + (last_quad(b) + 1) % 2][:, 128:256]
        m = b % 10

        def emit(e):
            e.matmul(P, aggT[:, b * 128:(b + 1) * 128], woT[:, :], start=True, stop=False)
            return e.matmul(P, one[0:1, 0:1].broadcast_to([1, 128]), bob[0:1, :], start=False, stop=True)
        at("tensor", "fo", 1, b, [("aa", min(last_quad(b) + 1, NQ - 1)), ("woT", None, 1), ("h0", b - 1),
                                  ("one", 0)], emit)
        at("vector", "h0", 1, b, [("fo", b)] + ([("n2", b - 10), ("od", group[b - 10])] if b >= 10 else []),
           lambda e: e.tensor_tensor(hb[:, m, :], P, xs[:, b, :], ALU.add))

    def project_stats(b):
        m = b % 10
        at("vector", "b1", 1, b, [("h0", b)], lambda e: e.bn_stats(st[:, 0, :], hb[:, m, :]))
        at("vector", "b2", 1, b, [("b1", b)], lambda e: e.bn_aggr(mv[:, 0, m, :], st[:, 0, :]))

    def root(g, n):
        lo, hi = span(g)
        at("scalar", f"q{n}", 1, g, [(f"b{2 * n}", groups[g][-1]), ("eps", 0)], lambda e: e.activation(
            sd[:, n - 1, lo:hi], mv[:, n - 1, lo:hi, 1], ACT.Sqrt, bias=epst[:, 0:1]))

    def inverse(g, n):
        lo, hi = span(g)
        at("vector", f"r{n}", 1, g, [(f"q{n}", g)], lambda e: e.reciprocal(sd[:, n - 1, lo:hi], sd[:, n - 1, lo:hi]))

    def norm1(b, part):
        g, m = group[b], b % 10
        y = hb[:, m, :]
        if part == 0:
            at("vector", "n1", 1, b, [("r1", g)], lambda e: e.scalar_tensor_tensor(
                y, y, mv[:, 0, m, 0:1], gab[:, :], ALU.subtract, ALU.mult))
        elif part == 1:
            at("vector", "g1", 1, b, [("n1", b)], lambda e: e.scalar_tensor_tensor(
                y, y, sd[:, 0, m:m + 1], xs[:, b, :], ALU.mult, ALU.add))
        elif part == 2:
            at("vector", "g2", 1, b, [("g1", b)], lambda e: e.tensor_tensor(y, y, beb[:, :], ALU.add))
        elif part == 3:
            at("vector", "b3", 1, b, [("g2", b)], lambda e: e.bn_stats(st[:, 1, :], y))
        else:
            at("vector", "b4", 1, b, [("b3", b)], lambda e: e.bn_aggr(mv[:, 1, m, :], st[:, 1, :]))

    def norm2(b):
        m = b % 10
        at("vector", "n2", 1, b, [("r2", group[b])], lambda e: e.tensor_scalar(
            hb[:, m, :], hb[:, m, :], mv[:, 1, m, 0:1], sd[:, 1, m:m + 1], ALU.subtract, ALU.mult))

    def store(g):
        lo, hi = span(g)
        b0 = groups[g][0] * 128
        if g < 5:
            at("sync", "od", 16, g, [("n2", groups[g][-1])], lambda e: e.dma_start(
                out[b0:b0 + (hi - lo) * 128, :].rearrange("(b p) c -> p b c", p=128), hb[:, lo:hi, :]))
        else:
            at("sync", "od", 16, 5, [("n2", 24)], lambda e: e.dma_start(out[b0:3072, :], hb[:, lo, :]))
            at("sync", "od", 16, 6, [("n2", 24)], lambda e: e.dma_start(out[3072:N, :], hb[0:53, lo + 1, :]))

    for k in range(PF):
        gathers(k)
    load_q(0)
    load_q(1)
    spread(0)
    spread(1)
    queries(0)
    first, begin = {}, 0
    for t in range(R * NB):
        begin = max(begin, last_quad(t // R) + 2 + t % R)
        first[begin] = t
        begin += 2 if t % R == R - 1 else 1
    second = {s + 1: t for s, t in first.items()}
    whole = {s + 2: t // R for s, t in first.items() if t % R == R - 1}
    known = {b: s for s, b in whole.items()}
    END = last_quad(NB - 1) + 3
    sums, c, s = [], 0, 0
    while c <= END:
        mine = []
        for n in range(2 if s >= CATCH and s % 8 in DOUBLE else 1):
            if s >= LAG and c <= END and known[last_block(min(c + 2, NQ - 1))] < s:
                mine.append(c)
                c += 1
        sums.append(mine)
        s += 1
    done, shown = {}, {}
    for s, mine in enumerate(sums):
        for c in mine:
            for b in range(NB):
                if c == last_quad(b) + 3:
                    done[c] = b
                    shown.setdefault(s + 1, []).append(b)
    todo, queue = {}, []
    for s in sorted(shown):
        for b in shown[s]:
            if b == groups[group[b]][-1]:
                queue.append((s, group[b]))
    free = 0
    for s, g in queue:
        n = len(groups[g])
        start = max(s + 1, free)
        late = g >= 4
        at_ = [start + 2 + m for m in range(n)] if late else [start + 1 + m for m in NORMS]
        todo.setdefault(start, []).append(lambda g=g: root(g, 1))
        todo.setdefault(start + 1, []).append(lambda g=g: inverse(g, 1))
        for m, k in enumerate(at_):
            todo.setdefault(k, []).append(("norm", groups[g][m]))
        k = at_[-1] + 1
        todo.setdefault(k, []).append(lambda g=g: root(g, 2))
        todo.setdefault(k + 1, []).append(lambda g=g: inverse(g, 2))
        for m, b in enumerate(groups[g]):
            k2 = k + 1 + (0 if late else m)
            todo.setdefault(k2, []).append(lambda b=b: norm2(b))
        todo.setdefault(k2, []).append(lambda g=g: store(g))
        free = k2 + 1

    def sum_front(c):
        if c == 0:
            load_c(0)
            load_c(1)
        if c < NQ:
            bring(c)
            shift(c)

    def ahead(c):
        if c + 2 < NQ:
            load_c(c + 2)

    def sum_end(c):
        if 0 <= c - 1 < NQ:
            gather_in(c - 1)
        if c in done:
            project(done[c])

    for s in range(max([len(sums), *todo, *whole]) + 1):
        mine = sums[s] if s < len(sums) else []
        c = mine[0] if mine else NQ + 9
        t, u = first.get(s), second.get(s)
        jobs = todo.get(s, [])
        w = [j[1] for j in jobs if isinstance(j, tuple)]
        if s + PF < NQ:
            gathers(s + PF)
        for b in range(NB):
            if min(last_quad(b) + FETCH, NQ - 1) == s + PF:
                fetch(b)
        if s + 2 < NQ:
            load_q(s + 2)
        sum_front(c)
        if s + 2 < NQ:
            spread(s + 2)
        if s + 1 < NQ:
            queries(s + 1)
        if 0 <= c - 1 < NQ:
            collect(c - 1)
        if s % 8 < 7 and s // 8 + 2 < NB:
            make_q(s // 8 + 2, s % 8)
        if u is not None:
            for part in (3, 4):
                maxima(u, part)
            exps(u)
        if s < NQ:
            logits(s, 0)
        for b in w:
            norm1(b, 0)
        if c < NQ:
            weigh(c, 0)
        if s < NQ:
            logits(s, 1)
        for b in w:
            norm1(b, 1)
        if c < NQ:
            weigh(c, 1)
        if s < NQ:
            logits(s, 2)
            logits(s, 3)
        ahead(c)
        for b in w:
            norm1(b, 2)
        if t is not None:
            maxima(t, 0)
        if c < NQ:
            weigh(c, 2)
        for b in w:
            norm1(b, 3)
        if t is not None:
            maxima(t, 1)
        sum_end(c)
        for b in w:
            norm1(b, 4)
        if t is not None:
            maxima(t, 2)
        for c in mine[1:]:
            sum_front(c)
            ahead(c)
            if 0 <= c - 1 < NQ:
                collect(c - 1)
            if c < NQ:
                for part in (0, 1, 2):
                    weigh(c, part)
            sum_end(c)
        for b in shown.get(s, []):
            project_stats(b)
        if s in whole:
            constants(whole[s])
        for j in jobs:
            if not isinstance(j, tuple):
                j()
    q.ends = [(f"lb{b}", last_quad(b) - first_quad(b) + 1) for b in range(NB)] + [("cw", NB), ("tq", NB - 2), ("tp", 2), ("od", 7)]




_INS = ["x", "src", "dst", "edge_type_5", "L0_gnn_W_Q", "L0_gnn_W_K", "L0_gnn_W_V", "L0_gnn_attn_bias",
        "L0_gnn_out_proj_w", "L0_gnn_out_proj_b", "L0_gnn_ln_gamma", "L0_gnn_ln_beta"]


def kernel(**inputs):
    import numpy as np
    import concourse.bacc as bacc
    from concourse.bass_utils import run_bass_kernel_spmd

    nc = bacc.Bacc("TRN2", target_bir_lowering=False, num_devices=1)
    arrays, args = {}, []
    for name in _INS:
        a = np.ascontiguousarray(inputs[name])
        arrays["in_" + name] = a
        args.append(nc.dram_tensor("in_" + name, a.shape, mybir.dt.from_np(a.dtype), kind="ExternalInput").ap())
    args.append(nc.dram_tensor("out_0", (N, C), F32, kind="ExternalOutput").ap())
    build(nc, *args)
    r = run_bass_kernel_spmd(nc, [arrays], core_ids=[0])
    return r.results[0]["out_0"]
```
